# Optimizing a Trainium2 kernel written in Bass

```python
import numpy as np
import jax
import jax.numpy as jnp

def _softmax(x, axis=-1):
    return jax.nn.softmax(x, axis=axis)

def _gelu(x):
    return jax.nn.gelu(x, approximate=True)

def _silu(x):
    return jax.nn.silu(x)

def _sigmoid(x):
    return jax.nn.sigmoid(x)

def _layernorm(x, axis=-1, eps=1e-05):
    m = jnp.mean(x, axis=axis, keepdims=True)
    v = jnp.var(x, axis=axis, keepdims=True)
    return (x - m) / jnp.sqrt(v + eps)

def _scatter_add(tgt, idx, src, axis=0):
    return tgt.at[idx].add(src)

def _segment_sum(src, seg, n):
    return jax.ops.segment_sum(src, seg, n)
kernel_name = 'mk_flamingo_gated_d1_seqx_r8_52c833'

def setup_inputs(seed: int=0):
    np.random.seed(seed)
    _w = jnp.asarray

    def _rec_inputs():
        import jax
        import jax.numpy as jnp
        _rk = jax.random.key(seed)
        x = 7.22e-05 + 1 * jax.random.normal(jax.random.fold_in(_rk, 1), (64, 64, 256), jnp.float32)
        _lenS = 64 - jax.random.randint(jax.random.fold_in(_rk, 7), (64,), 0, max(1, 64 // 4) + 1, jnp.int32)
        _lenS2 = 64 - jax.random.randint(jax.random.fold_in(_rk, 8), (64,), 0, max(1, 64 // 4) + 1, jnp.int32)
        _ctx_512P = jax.random.normal(jax.random.fold_in(_rk, 11), (64, 16, 64), jnp.float32)
        _ctx_512c = jax.random.dirichlet(jax.random.fold_in(_rk, 511), 0.3 * jnp.ones((16,), jnp.float32), (64, 64))
        _ctx_512t = jnp.einsum('bsk,bkd->bsd', _ctx_512c, _ctx_512P)
        _ctx_512t = _ctx_512t * jax.lax.rsqrt(jnp.mean(jnp.square(_ctx_512t)) + 1e-12) * 0.953939
        ctx_512 = -0.000514642 + 1.00011 * (_ctx_512t + 0.3 * jax.random.normal(jax.random.fold_in(_rk, 611), (64, 64, 64), jnp.float32))
        _g = jax.random.normal(jax.random.fold_in(_rk, 9001), (2, 1), jnp.float32)
        _g = jnp.sign(_g) * jnp.maximum(jnp.abs(_g), 1.0) + (_g == 0) * 1.0
        g_xattn = _g[0]
        g_ffn = _g[1]
        return (x, ctx_512, g_xattn, g_ffn)
    x, ctx_512, g_xattn, g_ffn = _rec_inputs()

    def _L0_xattn_setup():
        import jax, jax.numpy as jnp
        import numpy as np
        B, S, H, NH, L = (2, 256, 256, 16, 64)
        HD = H // NH
        key = jax.random.key(seed)
        k1, k2, k3, k4, k5 = jax.random.split(key, 5)
        scale = 0.02
        return {'q': jax.random.normal(k1, (B, S, H), dtype=jnp.float32), 'latent_kv': jax.random.normal(k2, (B, S, L), dtype=jnp.float32), 'Wq': jax.random.normal(k3, (H, H), dtype=jnp.float32) * scale, 'Wkv_expand': jax.random.normal(k4, (2 * H, L), dtype=jnp.float32) * scale, 'Wout': jax.random.normal(k5, (H, H), dtype=jnp.float32) * scale}
    _L0_xattn_all = _L0_xattn_setup()
    _L0_xattn_in = {k: v for k, v in _L0_xattn_all.items() if k in ('Wq', 'Wkv_expand', 'Wout')}
    del _L0_xattn_all

    def _L0_ffn_setup():
        import jax, jax.numpy as jnp
        import numpy as np
        from jax import lax
        D_MODEL = 256
        D_CROSS = 1024
        D_RETR = 128
        D_PRIV = 128
        N_EXPERTS = 2048
        N_HEADS = 8
        K_PER_HEAD = 8
        NUM_KEYS = int(np.sqrt(N_EXPERTS))
        BATCH, SEQ = (2, 256)
        key = jax.random.key(seed)
        ks = jax.random.split(key, 10)
        s = 0.02
        return {'hidden_states': jax.random.normal(ks[0], (BATCH, SEQ, D_MODEL), jnp.float32), 'W_up': jax.random.normal(ks[1], (D_CROSS, D_MODEL), jnp.float32) * s, 'b_up': jnp.zeros((D_CROSS,), jnp.float32), 'W_down': jax.random.normal(ks[2], (D_PRIV, D_CROSS), jnp.float32) * s, 'b_down': jnp.zeros((D_PRIV,), jnp.float32), 'W_q': jax.random.normal(ks[3], (D_RETR * N_HEADS, D_PRIV), jnp.float32) * s, 'keys': jax.random.normal(ks[4], (N_HEADS, NUM_KEYS, 2, D_RETR // 2), jnp.float32) * s, 'down_embed': jax.random.normal(ks[5], (N_EXPERTS, D_PRIV), jnp.float32) * s, 'up_embed': jax.random.normal(ks[6], (N_EXPERTS, D_MODEL), jnp.float32) * s}
    _L0_ffn_all = _L0_ffn_setup()
    _L0_ffn_in = {k: v for k, v in _L0_ffn_all.items() if k in ('W_up', 'b_up', 'W_down', 'b_down', 'W_q', 'keys', 'down_embed', 'up_embed')}
    del _L0_ffn_all
    return {'x': x, 'ctx_512': ctx_512, 'g_xattn': g_xattn, 'g_ffn': g_ffn, 'L0_xattn_Wq': _L0_xattn_in['Wq'], 'L0_xattn_Wkv_expand': _L0_xattn_in['Wkv_expand'], 'L0_xattn_Wout': _L0_xattn_in['Wout'], 'L0_ffn_W_up': _L0_ffn_in['W_up'], 'L0_ffn_b_up': _L0_ffn_in['b_up'], 'L0_ffn_W_down': _L0_ffn_in['W_down'], 'L0_ffn_b_down': _L0_ffn_in['b_down'], 'L0_ffn_W_q': _L0_ffn_in['W_q'], 'L0_ffn_keys': _L0_ffn_in['keys'], 'L0_ffn_down_embed': _L0_ffn_in['down_embed'], 'L0_ffn_up_embed': _L0_ffn_in['up_embed']}

def reference(x, ctx_512, g_xattn, g_ffn, L0_xattn_Wq, L0_xattn_Wkv_expand, L0_xattn_Wout, L0_ffn_W_up, L0_ffn_b_up, L0_ffn_W_down, L0_ffn_b_down, L0_ffn_W_q, L0_ffn_keys, L0_ffn_down_embed, L0_ffn_up_embed):
    import jax
    import jax.numpy as jnp

    def _L0_xattn_ref(q, latent_kv, Wq, Wkv_expand, Wout):
        import jax, jax.numpy as jnp
        import numpy as np
        B, S, H, NH, L = (2, 256, 256, 16, 64)
        HD = H // NH
        b, sq, _ = q.shape
        sk = latent_kv.shape[1]
        qp = q @ Wq.T
        kv = latent_kv @ Wkv_expand.T
        k, v = jnp.split(kv, 2, axis=-1)
        qh = qp.reshape(b, sq, NH, HD).transpose(0, 2, 1, 3)
        kh = k.reshape(b, sk, NH, HD).transpose(0, 2, 1, 3)
        vh = v.reshape(b, sk, NH, HD).transpose(0, 2, 1, 3)
        inv_sqrt_d = 1.0 / jnp.sqrt(jnp.float32(HD))
        scores = jnp.einsum('bhqd,bhkd->bhqk', qh, kh) * inv_sqrt_d
        causal = jnp.tril(jnp.ones((sq, sk), dtype=bool))
        scores = jnp.where(causal, scores, jnp.finfo(scores.dtype).min)
        attn = jax.nn.softmax(scores, axis=-1)
        out = jnp.einsum('bhqk,bhkd->bhqd', attn, vh)
        out = out.transpose(0, 2, 1, 3).reshape(b, sq, H)
        return out @ Wout.T

    def _L0_ffn_ref(hidden_states, W_up, b_up, W_down, b_down, W_q, keys, down_embed, up_embed):
        import jax, jax.numpy as jnp
        import numpy as np
        from jax import lax
        D_MODEL = 256
        D_CROSS = 1024
        D_RETR = 128
        D_PRIV = 128
        N_EXPERTS = 2048
        N_HEADS = 8
        K_PER_HEAD = 8
        NUM_KEYS = int(np.sqrt(N_EXPERTS))
        BATCH, SEQ = (2, 256)
        b, t, _ = hidden_states.shape
        act = jax.nn.silu
        h = act(jnp.einsum('btd,cd->btc', hidden_states, W_up) + b_up)
        h = jnp.einsum('btc,pc->btp', h, W_down) + b_down
        q = jnp.einsum('btp,rp->btr', h, W_q)
        q = q.reshape(b, t, 2, N_HEADS, D_RETR // 2).transpose(2, 0, 1, 3, 4)
        sim = jnp.einsum('pbthn,hkpn->pbthk', q, keys)
        scores, idx = lax.top_k(sim, K_PER_HEAD)
        sx, sy = (scores[0], scores[1])
        ix, iy = (idx[0], idx[1])
        all_scores = (sx[..., :, None] + sy[..., None, :]).reshape(b, t, N_HEADS, K_PER_HEAD * K_PER_HEAD)
        all_indices = (ix[..., :, None] * NUM_KEYS + iy[..., None, :]).reshape(b, t, N_HEADS, K_PER_HEAD * K_PER_HEAD)
        sc, pk = lax.top_k(all_scores, K_PER_HEAD)
        indices = jnp.take_along_axis(all_indices, pk, axis=-1)
        de = down_embed[indices]
        ue = up_embed[indices]
        z = jnp.einsum('btd,bthkd->bthk', h, de)
        z = act(z * jax.nn.softmax(sc, axis=-1))
        out = jnp.einsum('bthk,bthkd->btd', z, ue)
        return out
    x = x + jnp.tanh(g_xattn[0]) * _L0_xattn_ref(_layernorm(x, axis=-1), ctx_512, L0_xattn_Wq, L0_xattn_Wkv_expand, L0_xattn_Wout)
    x = x + jnp.tanh(g_ffn[0]) * _L0_ffn_ref(_layernorm(x, axis=-1), L0_ffn_W_up, L0_ffn_b_up, L0_ffn_W_down, L0_ffn_b_down, L0_ffn_W_q, L0_ffn_keys, L0_ffn_down_embed, L0_ffn_up_embed)
    return x

_drawn_inputs = setup_inputs


def setup_inputs(seed=0):
    import zlib

    import numpy as np

    out = dict(_drawn_inputs(seed))
    spreads = {'L0_ffn_b_up': (0.0, 0.8), 'L0_ffn_b_down': (0.0, 0.8)}
    factors = {'ctx_512': 2.803,
     'L0_xattn_Wq': 8.0,
     'L0_ffn_W_up': 8.0,
     'L0_ffn_W_down': 8.0,
     'L0_ffn_W_q': 8.0,
     'L0_ffn_keys': 8.0,
     'L0_ffn_down_embed': 8.0,
     'L0_ffn_up_embed': 8.0}
    for name, (base, spread) in spreads.items():
        noise = np.random.default_rng([zlib.crc32(name.encode()), seed]).standard_normal(out[name].shape)
        drawn = base * np.exp(spread * noise) if base else spread * noise
        out[name] = jnp.asarray(drawn.astype(out[name].dtype))
    for name, factor in factors.items():
        out[name] = (out[name] * factor).astype(out[name].dtype)
    return out
```

```python
import concourse.bass as bass
from concourse import mybir
from contextlib import ExitStack

TOKENS, DM, CTX = 4096, 256, 64
SEQ, HEADS, HD = 64, 16, 16
DUP, DP = 1024, 128
RH, NK, K8 = 8, 45, 8
SLOTS = RH * K8
NE, R = 2048, 128
C = NE // R
TILE = 128
TILES = TOKENS // TILE
Q = TILE // 2
EPS = 1e-5
MASKED = -1e30


def flamingo_layer(nc, x, ctx_512, g_xattn, g_ffn, Wq, Wkv, Wout, W_up, b_up, W_down, b_down, W_r,
                   keys, down_embed, up_embed, out):
    F, H, U = mybir.dt.float32, mybir.dt.bfloat16, mybir.dt.uint32
    ALU, ACT, AX = mybir.AluOpType, mybir.ActivationFunctionType, mybir.AxisListType

    x_d = x.rearrange("b s d -> (b s) d").rearrange("(t p) d -> t p d", p=TILE)
    ctx_d = ctx_512.rearrange("b s d -> (b s) d").rearrange("(t p) d -> t p d", p=TILE)
    out_d = out.rearrange("b s d -> (b s) d").rearrange("(t p) d -> t p d", p=TILE)
    rows_d = nc.dram_tensor("expert_rows", (2, Q, 2, SLOTS), H, kind="Internal").ap()

    es = ExitStack()
    with es:
        def sb(name, shape, dt=F):
            return es.enter_context(nc.sbuf_tensor(name, shape, dt))

        def sem(name):
            return es.enter_context(nc.semaphore(name))

        ident = sb("ident", [128, 128])
        ident_h = sb("ident_h", [128, 128], H)
        causal = sb("causal", [128, 8, SEQ], H)
        head_of = sb("head_of", [128, 8])
        col_iota = sb("col_iota", [128, R, 16], H)
        a_iota = sb("a_iota", [128, K8], F)
        p_iota = sb("p_iota", [128, 1])
        minus_half = sb("minus_half", [128, 1])
        gates = sb("gates", [128, 2])
        bup_sb = sb("bup_sb", [128, DUP // 128])
        bdn_sb = sb("bdn_sb", [128, 1])
        WqT = sb("WqT", [128, 2, DM])
        WkvT = sb("WkvT", [CTX, 2 * DM])
        WoT = sb("WoT", [128, 2, DM])
        WupT = sb("WupT", [128, 2, DUP])
        WdT = sb("WdT", [128, DUP // 128, DP])
        simW = sb("simW", [DP, 2, RH * NK])
        deT = sb("deT", [DP, NE])
        ue = sb("ue", [R, C, DM])

        xt = sb("xt", [128, 2, DM])
        ct = sb("ct", [128, 2, CTX])
        st6 = sb("st6", [128, 6])
        mv = sb("mv", [128, 2])
        veps = sb("veps", [128, 1])
        rstd = sb("rstd", [128, 1])
        st6b = sb("st6b", [128, 6])
        mvb = sb("mvb", [128, 2])
        vepsb = sb("vepsb", [128, 1])
        rstdb = sb("rstdb", [128, 1])
        xn = sb("xn", [128, DM])
        xnT = sb("xnT", [128, 2, TILE])
        ctxT = sb("ctxT", [CTX, 2, 2, SEQ])
        qT = sb("qT", [128, 2, TILE])
        kT = sb("kT", [128, 2, TILE])
        k_diag = sb("k_diag", [128, 2, 2, 8, SEQ])
        v_diag = sb("v_diag", [128, 2, 8, 2, HD + 1])
        smax = sb("smax", [128, HEADS])
        P = sb("P", [128, HEADS, SEQ])
        PT = sb("PT", [128, 8, TILE])
        rsum = sb("rsum", [128, 8, 2, 1])
        oT = sb("oT", [128, 2, TILE])
        x1 = sb("x1", [128, 2, DM])
        xn2T = sb("xn2T", [128, 2, TILE])
        up_pre = P[:, :, :].rearrange("p h k -> p (h k)").rearrange("p (a t) -> p a t", a=8)
        up_t = PT
        up_act = sb("up_act", [128, 8, TILE])
        hT = sb("hT", [DP, TILE])
        sims = sb("sims", [128, 2 * RH, NK])
        z = sb("z", [R, 2, C, TILE])
        zl = sb("zl", [R, 2, C, TILE])
        zll = sb("zll", [R, 2, C, TILE], H)

        x1k = sb("x1k", [128, 2, DM])
        top = sb("top", [128, 2 * RH, K8])
        topi = sb("topi", [128, 2 * RH, K8], U)
        topf = sb("topf", [128, 2 * RH, K8])
        sums = sb("sums", [128, RH, K8, K8])
        best = sb("best", [128, RH, K8])
        besti = sb("besti", [128, RH, K8], U)
        ab_i = sb("ab_i", [128, 2, SLOTS], U)
        ab_f = sb("ab_f", [128, 2, SLOTS])
        eq = sb("eq", [128, 2, SLOTS, K8])
        xy = sb("xy", [128, 2, SLOTS])
        e_i = sb("e_i", [128, SLOTS], U)
        rc_i = sb("rc_i", [128, 2, SLOTS], U)
        r_h = sb("r_h", [128, SLOTS], H)
        sm_in = sb("sm_in", [128, 3, 2, SLOTS])
        dif = sb("dif", [128, RH, K8])
        ex = sb("ex", [128, RH, K8])
        exs = sb("exs", [128, RH, 1])
        exr = sb("exr", [128, RH, 1])
        rc_sm = sb("rc_sm", [128, 2, 2, Q], H)
        p_sm = sb("p_sm", [128, 2, Q])

        hot_rT = sb("hot_rT", [R, Q, 2 * SLOTS], H)
        hot_r = sb("hot_r", [128, R, Q], H)
        hot_c = sb("hot_c", [128, 2 * C, Q], H)
        picked = sb("picked", [128, 2, 16, 2 * C])
        zs = sb("zs", [128, Q])
        zp = sb("zp", [128, Q])
        zt = sb("zt", [128, Q])
        u = sb("u", [128, Q])
        u_l = sb("u_l", [128, Q])
        u_ll = sb("u_ll", [128, Q])
        u_h = sb("u_h", [128, 3, Q], H)
        uc = sb("uc", [128, 3, 2 * C, Q], H)
        coef = sb("coef", [R, C, 2, Q])

        banks = [es.enter_context(nc.psum_tensor(f"bank{i}", [128, 512], F)) for i in range(8)]
        bT, bD, bG0, bG1, bS0, bS1, bP0, bP1 = banks
        bG, bS, bP = (bG0, bG1), (bS0, bS1), (bP0, bP1)

        wq_n = P[:, 0:8, :].rearrange("p h k -> p (h k)").rearrange("p (a k) -> p a k", a=2)
        wo_n = P[:, 8:16, :].rearrange("p h k -> p (h k)").rearrange("p (a k) -> p a k", a=2)
        wkv_n = PT[:, 0:2, :].rearrange("p a b -> p (a b)").rearrange("p (a k) -> p a k", a=4)
        wup_n = z[:, 0, :, :].rearrange("p c t -> p (c t)").rearrange("p (a k) -> p a k", a=8)
        wdn_n = z[:, 1, 0:8, :].rearrange("p a t -> p (a t)")
        wr_n = zl[:, 1, 0:8, :]
        keys_n = up_act
        de_n = zl[:, 0, :, :]
        keysT = k_diag[:, 0, 0, :, 0:NK]

        S = {n: sem(n) for n in (
            "wq_in wo_in wkv_in wup_in wdn_in wr_in keys_in de_in ue_in small_in "
            "const_step consts gate_done wT_pe wT_dve simw_pe simw_done "
            "x_in0 x_in1 ctx_in0 ctx_in1 stats stats2 eps_ok rstd_ok xn_ok xT_pe xT_sb ctxT_sb q_pe v_pe q_sb k_sb v_sb0 v_sb1 "
            "kdiag0 kdiag1 s_pe0 s_pe1 max0 max1 sub0 sub1 exp0 exp1 pt_pe0 pt_pe1 pt_sb0 pt_sb1 av_pe rs_ok o_ok "
            "oT_pe oT_sb wo_pe x1_ok lstats lstats2 leps_ok lrstd_ok xn2_ok x2T_pe x2T_sb up_pe0 up_pe1 pre0 pre1 tanh0 tanh1 "
            "act0 act1 hid_pe hid_sb sim_pe0 sim_pe1 sim_sb0 sim_sb1 z_pe0 z_pe1 z_pe2 z_pe3 z_sb0 z_sb1 z_sb2 z_sb3 "
            "zl_ok zll_ok "
            "x1k_ok top_v top_i topf_ok sums_ok best_v best_i a_ok b_ok ab_ok eq_ok pick_ok xy_ok e_ok rci_ok rh_ok rdup_ok "
            "dif_ok ex_ok exs_ok exr_ok p_ok sm_pe sm_rc sm_p rows_out "
            "rows_in hotrT hotr hotc g_pe0 g_pe1 g_pe2 g_pe3 gm0 gm1 gm2 gm3 zs0 zs1 zs2 zs3 zp_ok zt_ok u_ok uh1 ul_ok uh2 ull_ok uh3 "
            "uc0 uc1 uc2 w_pe0 w_pe1 w_pe2 w_pe3 w_sb0 w_sb1 w_sb2 w_sb3 out_pe y_ok y_out0 y_out1 settled"
        ).split()}

        class Turn:

            def __init__(self, eng, t, pair):
                self.eng, self.t, self.pair = eng, t, pair
                self.now, self.prev = (t + 1 if isinstance(t, int) else eng.snap(t + 1)), t

            def wait(self, name):
                self.eng.wait_ge(S[name], self.now)

            def wait_apart(self, name):
                self.wait(name)
                self.eng.sem_inc(S["settled"], 1)

            def wait_dma(self, name, n=1):
                self.eng.wait_ge(S[name], 16 * n * (self.t + 1))

            def wait_dma_side(self, name):
                self.eng.wait_ge(S[name], 16 * (self.pair + 1))

            def free_dma_side(self, name):
                if not isinstance(self.pair, int) or self.pair > 0:
                    self.eng.wait_ge(S[name], 16 * self.pair)

            def free(self, name):
                if not isinstance(self.prev, int) or self.prev > 0:
                    self.eng.wait_ge(S[name], self.prev)

            def free2(self, name):
                v = self.t - 1
                if not isinstance(v, int) or v > 0:
                    self.eng.wait_ge(S[name], v)

        def pipeline(eng, turn):
            turn(Turn(eng, 0, 0), None, None, 0)
            turn(Turn(eng, 1, 0), Turn(eng, 0, 0), None, 1)
            turn(Turn(eng, 2, 1), Turn(eng, 1, 0), Turn(eng, 0, 0), 0)
            turn(Turn(eng, 3, 1), Turn(eng, 2, 1), Turn(eng, 1, 0), 1)
            with eng.Fori(2, TILES // 2) as pair:
                first = eng.snap(pair * 2)
                turn(Turn(eng, first, pair), Turn(eng, eng.snap(first - 1), pair - 1), Turn(eng, eng.snap(first - 2), pair - 1), 0)
                turn(Turn(eng, eng.snap(first + 1), pair), Turn(eng, first, pair), Turn(eng, eng.snap(first - 1), pair - 1), 1)
            turn(None, Turn(eng, TILES - 1, TILES // 2 - 1), Turn(eng, TILES - 2, TILES // 2 - 1), 0)
            turn(None, None, Turn(eng, TILES - 1, TILES // 2 - 1), 1)

        def top_half(ap):
            return ap.bitcast(H)[:, :, 1::2]

        def weight_groups():
            yield "wq_in", [wq_n[:, o, k * 128:k * 128 + 128] for k in range(2) for o in range(2)], \
                WqT[:, :, :].rearrange("p k (o m) -> p (k o) m", o=2), 1.0
            yield "wkv_in", [wkv_n[:, o, :] for o in range(4)], WkvT[:, :].rearrange("p (o m) -> p o m", o=4), 1.0
            yield "wo_in", [wo_n[:, o, k * 128:k * 128 + 128] for k in range(2) for o in range(2)], \
                WoT[:, :, :].rearrange("p k (o m) -> p (k o) m", o=2), 1.0
            for k in range(2):
                for g in range(2):
                    yield "wup_in", [wup_n[:, 4 * g + o, k * 128:k * 128 + 128] for o in range(4)], \
                        WupT[:, k, 512 * g:512 * g + 512].rearrange("p (o m) -> p o m", o=4), 1.0
            for g in range(2):
                yield "wdn_in", [wdn_n[:, 128 * (4 * g + o):128 * (4 * g + o) + 128] for o in range(4)], \
                    WdT[:, 4 * g:4 * g + 4, :], 0.5
            for g in range(4):
                yield "de_in", [de_n[:, 4 * g + o, :] for o in range(4)], \
                    deT[:, 512 * g:512 * g + 512].rearrange("p (o m) -> p o m", o=4), 1.0
            for g in range(2):
                yield "keys_in", [keys_n[0:NK, 4 * g + o, :] for o in range(4)], keysT[:, 4 * g:4 * g + 4, :], 1.0

        block = es.enter_context(nc.Block())

        @block.sync
        def _(sp):
            sp.dma_start(wq_n, Wq.rearrange("(a p) k -> p a k", p=128)).then_inc(S["wq_in"], 16)
            sp.dma_start(wkv_n, Wkv.rearrange("(a p) k -> p a k", p=128)).then_inc(S["wkv_in"], 16)
            sp.dma_start(bup_sb[:, :], b_up.rearrange("(a p) -> p a", p=128), allow_slow_non_contiguous=True).then_inc(S["small_in"], 16)
            sp.dma_start(bdn_sb[:, :], b_down.rearrange("(p a) -> p a", a=1)).then_inc(S["small_in"], 16)
            sp.dma_start(gates[:, 0:1], g_xattn.rearrange("(a b) -> a b", b=1).to_broadcast([128, 1])).then_inc(S["small_in"], 16)
            sp.dma_start(gates[:, 1:2], g_ffn.rearrange("(a b) -> a b", b=1).to_broadcast([128, 1])).then_inc(S["small_in"], 16)
            sp.dma_start(wo_n, Wout.rearrange("(a p) k -> p a k", p=128)).then_inc(S["wo_in"], 16)
            sp.dma_start(wup_n, W_up.rearrange("(a p) k -> p a k", p=128)).then_inc(S["wup_in"], 16)
            sp.dma_start(wdn_n, W_down).then_inc(S["wdn_in"], 16)
            for s in range(2):
                sp.dma_start(wr_n[s * 64:s * 64 + 64, :, :],
                             W_r[s * 512:s * 512 + 512, :].rearrange("(h n) p -> n h p", n=64)).then_inc(S["wr_in"], 16)
            sp.dma_start(keys_n[0:NK, :, :].rearrange("k h (s n) -> k h s n", s=2),
                         keys.rearrange("h k s n -> k h s n")).then_inc(S["keys_in"], 16)
            sp.dma_start(de_n, down_embed.rearrange("(c r) d -> r c d", r=R)).then_inc(S["de_in"], 16)
            sp.dma_start(ue[:, :, :], up_embed.rearrange("(c r) d -> r c d", r=R)).then_inc(S["ue_in"], 16)

            def turn(A, B, Ct, side):
                if A:
                    A.free2("x1_ok")
                    sp.dma_start(xt[:, side, :], x_d[bass.ds(A.t, 1), :, :].rearrange("a p d -> p (a d)")).then_inc(S[f"x_in{side}"], 16)
                    A.free2("xT_pe")
                    sp.dma_start(ct[:, side, :], ctx_d[bass.ds(A.t, 1), :, :].rearrange("a p d -> p (a d)")).then_inc(S[f"ctx_in{side}"], 16)
                if B:
                    b = 1 - side
                    B.wait("rh_ok")
                    for half in range(2):
                        sp.dma_start(rows_d[b, :, half, :], r_h[half * Q:half * Q + Q, :]).then_inc(S["rows_out"], 16)
                    B.wait_dma("rows_out", 2)
                    B.free("g_pe3")
                    sp.dma_start(hot_rT[:, :, :].rearrange("r q s -> r (q s)"),
                                 rows_d[b:b + 1, :, :, :].rearrange("b q h s -> b (q h s)").to_broadcast([128, Q * 2 * SLOTS]),
                                 ).then_inc(S["rows_in"], 16)
                if Ct:
                    Ct.wait("y_ok")
                    sp.dma_start(out_d[bass.ds(Ct.t, 1), :, :].rearrange("a p d -> p (a d)"), x1k[:, side, :]).then_inc(S[f"y_out{side}"], 16)

            pipeline(sp, turn)
            for side in range(2):
                sp.wait_ge(S[f"y_out{side}"], 16 * (TILES // 2))

        @block.gpsimd
        def _(pool):
            steps = [0]

            def step(ins):
                ins.then_inc(S["const_step"], 1)
                steps[0] += 1
                pool.wait_ge(S["const_step"], steps[0])

            small = dict(allow_small_or_imprecise_dtypes=True)
            step(nc.gpsimd.memset(ident[:, :], 0.0))
            step(nc.gpsimd.memset(causal[:, :, :], 0.0))
            step(nc.gpsimd.memset(head_of[:, :], 1.0))
            step(nc.gpsimd.memset(v_diag[:, :, :, :, :], 0.0))
            step(nc.gpsimd.memset(minus_half[:, :], -0.5))
            step(nc.gpsimd.iota(col_iota[:, :, :], pattern=[[1, R], [0, 16]], base=0, channel_multiplier=0, **small))
            step(nc.gpsimd.iota(a_iota[:, :], pattern=[[1, K8]], base=0, channel_multiplier=0, **small))
            step(nc.gpsimd.iota(p_iota[:, :], pattern=[[0, 1]], base=0, channel_multiplier=1, **small))
            step(nc.gpsimd.affine_select(out=ident[:, :], in_=ident[:, :], compare_op=ALU.not_equal, fill=1.0,
                                         base=0, pattern=[[-1, 128]], channel_multiplier=1))
            for s in range(2):
                rows = causal[s * SEQ:s * SEQ + SEQ, :, :]
                step(nc.gpsimd.affine_select(out=rows, in_=rows, compare_op=ALU.is_ge, fill=MASKED,
                                             base=0, pattern=[[0, 8], [-1, SEQ]], channel_multiplier=1))
            for odd in range(2):
                step(nc.gpsimd.memset(v_diag[odd * 64:odd * 64 + 64, :, :, odd, HD:HD + 1], 1.0))
            step(nc.gpsimd.affine_select(out=head_of[:, :], in_=head_of[:, :], compare_op=ALU.is_ge, fill=0.0,
                                         base=0, pattern=[[-HD, 8]], channel_multiplier=1))
            step(nc.gpsimd.affine_select(out=head_of[:, :], in_=head_of[:, :], compare_op=ALU.is_ge, fill=0.0,
                                         base=HD - 1, pattern=[[HD, 8]], channel_multiplier=-1))
            nc.gpsimd.tensor_copy(ident_h[:, :], ident[:, :]).then_inc(S["consts"], 1)
            pool.wait_ge(S["simw_done"], 1)

            def turn(A, B, Ct, side):
                if A:
                    A.wait("eps_ok")
                    nc.gpsimd.tensor_tensor(rstd[:, :], veps[:, :], minus_half[:, :], ALU.pow).then_inc(S["rstd_ok"], 1)
                if A:
                    for half in range(2):
                        A.wait("k_sb")
                        A.free(f"s_pe{half}")
                        nc.gpsimd.tensor_tensor(
                            k_diag[:, half, :, :, :],
                            kT[:, half, :].rearrange("p (b k) -> p b k", b=2).unsqueeze(2).to_broadcast([128, 2, 8, SEQ]),
                            head_of[:, :].unsqueeze(1).unsqueeze(3).to_broadcast([128, 2, 8, SEQ]),
                            ALU.mult).then_inc(S[f"kdiag{half}"], 1)
                if Ct:
                    for n, ready in ((2, "uh3"),):
                        Ct.wait("hotc")
                        Ct.wait(ready)
                        Ct.free("w_pe3")
                        nc.gpsimd.tensor_tensor(uc[:, n, :, :], hot_c[:, :, :],
                                                u_h[:, n:n + 1, :].to_broadcast([128, 2 * C, Q]), ALU.mult).then_inc(S[f"uc{n}"], 1)
                if B:
                    b = 1 - side
                    B.wait("x1_ok")
                    B.free_dma_side(f"y_out{b}")
                    pool.sem_inc(S["settled"], 1)
                    nc.gpsimd.tensor_copy(x1k[:, b, :], x1[:, b, :]).then_inc(S["x1k_ok"], 1)
                if A:
                    A.wait("leps_ok")
                    nc.gpsimd.tensor_tensor(rstdb[:, :], vepsb[:, :], minus_half[:, :], ALU.pow).then_inc(S["lrstd_ok"], 1)
                if B:
                    B.wait("z_sb3")
                    B.free2("g_pe3")
                    nc.gpsimd.tensor_tensor(zl[:, b, :, :], z[:, b, :, :], top_half(z[:, b, :, :]), ALU.subtract).then_inc(S["zl_ok"], 1)
                    B.wait("zl_ok")
                    nc.gpsimd.tensor_tensor(zll[:, b, :, :], zl[:, b, :, :], top_half(zl[:, b, :, :]), ALU.subtract).then_inc(S["zll_ok"], 1)

            pipeline(pool, turn)

        @block.scalar
        def _(act):
            act.wait_ge(S["small_in"], 64)
            nc.scalar.activation(gates[:, :], gates[:, :], ACT.Tanh).then_inc(S["gate_done"], 1)
            act.wait_ge(S["simw_done"], 1)

            def turn(A, B, Ct, side):
                def copy(dst, src, done, scale=1.0):
                    nc.scalar.activation(dst, src, ACT.Copy, scale=scale).then_inc(S[done], 1)

                def coef_copy(k):
                    Ct.wait(f"w_pe{k}")
                    if k == 0:
                        Ct.free("out_pe")
                    copy(coef[:, :, :, 16 * k:16 * k + 16].rearrange("r c h q -> r q h c"),
                         bG[k % 2][:, :].rearrange("r (q h c) -> r q h c", q=16, h=2), f"w_sb{k}")

                if A:
                    A.wait("xT_pe")
                    A.free("q_pe")
                    copy(xnT[:, :, :], bT[:, 0:256].rearrange("p (a t) -> p a t", a=2), "xT_sb")
                    A.free("v_pe")
                    copy(ctxT[:, :, :, :], bT[0:CTX, 256:384].rearrange("l (b k) -> l b k", b=2)
                         .unsqueeze(2).to_broadcast([CTX, 2, 2, SEQ]), "ctxT_sb")
                    A.wait("q_pe")
                    A.free("s_pe1")
                    copy(qT[:, :, :], bD[:, 0:256].rearrange("p (a t) -> p a t", a=2), "q_sb")
                    A.free("kdiag1")
                    copy(kT[:, :, :], bD[:, 256:512].rearrange("p (a t) -> p a t", a=2), "k_sb")
                    A.wait("v_pe")
                    A.free("av_pe")
                    for odd in range(2):
                        rows = slice(odd * 64, odd * 64 + 64)
                        copy(v_diag[rows, :, :, odd, 0:HD],
                             bP0[rows, :].rearrange("k (b h o d) -> k b h o d", b=2, h=8, o=2)[:, :, :, odd, :], f"v_sb{odd}")
                if A:
                    for half in range(2):
                        A.wait(f"sub{half}")
                        hs = slice(8 * half, 8 * half + 8)
                        nc.scalar.activation(P[:, hs, :], P[:, hs, :], ACT.Exp, scale=HD ** -0.5).then_inc(S[f"exp{half}"], 1)
                if Ct:
                    Ct.wait("zp_ok")
                    nc.scalar.activation(zt[:, :], zp[:, :], ACT.Tanh, scale=0.5).then_inc(S["zt_ok"], 1)
                if A:
                    for n in range(2):
                        A.wait(f"pt_pe{n}")
                        A.free("act1")
                        copy(PT[:, 4 * n:4 * n + 4, :], bP[n][:, :].rearrange("p (a t) -> p a t", a=4), f"pt_sb{n}")
                    A.wait("oT_pe")
                    A.free("wo_pe")
                    copy(oT[:, :, :], bT[:, 0:256].rearrange("p (a t) -> p a t", a=2), "oT_sb")
                if B:
                    B.wait("dif_ok")
                    B.free("p_ok")
                    nc.scalar.activation(ex[:, :, :], dif[:, :, :], ACT.Exp).then_inc(S["ex_ok"], 1)
                if Ct:
                    coef_copy(0)
                    coef_copy(1)
                    coef_copy(2)
                if A:
                    A.wait("x2T_pe")
                    A.free("up_pe1")
                    copy(xn2T[:, :, :], bT[:, 0:256].rearrange("p (a t) -> p a t", a=2), "x2T_sb")
                if Ct:
                    coef_copy(3)
                if A:
                    for n in range(2):
                        A.wait(f"up_pe{n}")
                        for m in range(4):
                            c = 4 * n + m
                            last = nc.scalar.activation(up_pre[:, c, :], bS[n][:, 128 * m:128 * m + 128], ACT.Identity,
                                                        bias=bup_sb[:, c:c + 1])
                        last.then_inc(S[f"pre{n}"], 1)
                        A.wait(f"pre{n}")
                        nc.scalar.activation(up_t[:, 4 * n:4 * n + 4, :], up_pre[:, 4 * n:4 * n + 4, :], ACT.Tanh,
                                             scale=0.5).then_inc(S[f"tanh{n}"], 1)
                    A.wait("hid_pe")
                    A.free("z_pe3")
                    nc.scalar.activation(hT[:, :], bD[:, 0:TILE], ACT.Identity, bias=bdn_sb[:, 0:1]).then_inc(S["hid_sb"], 1)
                    A.free("top_i")
                    for s in range(2):
                        A.wait(f"sim_pe{s}")
                        copy(sims[:, RH * s:RH * s + RH, :], bP[s][:, 0:RH * NK].rearrange("t (h k) -> t h k", h=RH), f"sim_sb{s}")
                    A.free2("g_pe3")
                    A.free2("zll_ok")
                    for n in range(4):
                        A.wait(f"z_pe{n}")
                        copy(z[:, side, 4 * n:4 * n + 4, :], bS[n % 2][:, :].rearrange("r (c t) -> r c t", c=4), f"z_sb{n}")

            pipeline(act, turn)

        @block.vector
        def _(dve):
            for n, (_, srcs, dst, scale) in enumerate(weight_groups()):
                dve.wait_ge(S["wT_pe"], n + 1)
                rows, w = srcs[0].shape[1], srcs[0].shape[0]
                src = banks[n % 8][0:rows, :].rearrange("p (a w) -> p a w", w=128)[:, 0:len(srcs), 0:w]
                if scale == 1.0:
                    nc.vector.tensor_copy(dst, src).then_inc(S["wT_dve"], 1)
                else:
                    nc.vector.tensor_scalar(dst, src, scale, None, ALU.mult).then_inc(S["wT_dve"], 1)
            dve.wait_ge(S["simw_pe"], 1)
            for s in range(2):
                last = nc.vector.tensor_copy(simW[:, s, :], banks[s][:, 0:RH * NK])
            last.then_inc(S["simw_done"], 1)
            dve.wait_ge(S["consts"], 1)
            dve.wait_ge(S["gate_done"], 1)

            def turn(A, B, Ct, side):
                b = 1 - side

                def gathered(k):
                    Ct.wait(f"g_pe{k}")
                    Ct.wait("hotc")
                    nc.vector.tensor_tensor(picked[:, k % 2, :, :], bG[k % 2][:, :].rearrange("s (q c) -> s q c", q=16),
                                            hot_c[:, :, 16 * k:16 * k + 16].rearrange("s c q -> s q c"), ALU.mult).then_inc(S[f"gm{k}"], 1)

                def gathered_sum(k):
                    Ct.wait(f"gm{k}")
                    nc.vector.tensor_reduce(zs[:, 16 * k:16 * k + 16], picked[:, k % 2, :, :], AX.X, ALU.add).then_inc(S[f"zs{k}"], 1)

                def scores_max(half):
                    hs = slice(8 * half, 8 * half + 8)
                    s3 = bS[half][:, :].rearrange("p (h k) -> p h k", h=8)
                    A.wait(f"s_pe{half}")
                    nc.vector.reduce_max(smax[:, hs], s3, AX.X).then_inc(S[f"max{half}"], 1)
                    A.wait(f"max{half}")
                    A.free("act1")
                    nc.vector.tensor_tensor(P[:, hs, :], s3, smax[:, hs].unsqueeze(2).to_broadcast([128, 8, SEQ]),
                                            ALU.subtract).then_inc(S[f"sub{half}"], 1)

                if A:
                    A.wait_dma_side(f"x_in{side}")
                    nc.vector.bn_stats(st6[:, :], xt[:, side, :]).then_inc(S["stats"], 1)
                    A.wait_apart("stats")
                    nc.vector.bn_aggr(mv[:, :], st6[:, :]).then_inc(S["stats2"], 1)
                    A.wait("stats2")
                    nc.vector.tensor_scalar(veps[:, :], mv[:, 1:2], EPS, None, ALU.add).then_inc(S["eps_ok"], 1)
                if Ct:
                    Ct.wait_dma("rows_in")
                    nc.vector.tensor_scalar(hot_rT[:, :, :], hot_rT[:, :, :], p_iota[:, 0:1], None, ALU.is_equal).then_inc(S["hotrT"], 1)
                    Ct.wait("sm_rc")
                    Ct.free("uc2")
                    nc.vector.tensor_tensor(
                        hot_c[:, :, :].rearrange("s c (a q) -> s a c q", q=16),
                        rc_sm[:, side, 1, :].rearrange("s (a q) -> s a q", q=16).unsqueeze(2).to_broadcast([128, 4, 2 * C, 16]),
                        col_iota[:, 0:2 * C, :].unsqueeze(1).to_broadcast([128, 4, 2 * C, 16]), ALU.is_equal).then_inc(S["hotc"], 1)
                if A:
                    A.wait("rstd_ok")
                    A.free("x2T_pe")
                    nc.vector.tensor_scalar(xn[:, :], xt[:, side, :], mv[:, 0:1], rstd[:, 0:1], ALU.subtract, ALU.mult).then_inc(S["xn_ok"], 1)
                if B:
                    B.wait_apart("sim_sb1")
                    for l in range(2 * RH):
                        last = nc.vector.max(top[:, l, :], sims[:, l, :])
                    last.then_inc(S["top_v"], 1)
                    B.wait_apart("top_v")
                    for l in range(2 * RH):
                        last = nc.vector.max_index(topi[:, l, :], top[:, l, :], sims[:, l, :])
                    last.then_inc(S["top_i"], 1)
                if Ct:
                    for k in range(2):
                        gathered(k)
                        gathered_sum(k)
                if A:
                    scores_max(0)
                    scores_max(1)
                if Ct:
                    for k in range(2, 4):
                        gathered(k)
                        gathered_sum(k)
                    Ct.wait("zs3")
                    Ct.wait("sm_p")
                    nc.vector.tensor_tensor(zp[:, :], zs[:, :], p_sm[:, side, :], ALU.mult).then_inc(S["zp_ok"], 1)
                if B:
                    nc.vector.tensor_tensor(sums[:, :, :, :],
                                            top[:, 0:RH, :].unsqueeze(3).to_broadcast([128, RH, K8, K8]),
                                            top[:, RH:2 * RH, :].unsqueeze(2).to_broadcast([128, RH, K8, K8]), ALU.add).then_inc(S["sums_ok"], 1)
                    B.wait("top_i")
                    nc.vector.tensor_copy(topf[:, :, :], topi[:, :, :]).then_inc(S["topf_ok"], 1)
                    B.wait_apart("sums_ok")
                    for h in range(RH):
                        last = nc.vector.max(best[:, h, :], sums[:, h, :, :].rearrange("p a b -> p (a b)"))
                    last.then_inc(S["best_v"], 1)
                if Ct:
                    Ct.wait("zt_ok")
                    nc.vector.scalar_tensor_tensor(u[:, :], zt[:, :], 1.0, zp[:, :], ALU.add, ALU.mult).then_inc(S["u_ok"], 1)
                    Ct.wait("u_ok")
                    nc.vector.tensor_scalar(u[:, :], u[:, :], 0.5, None, ALU.mult).then_inc(S["uh1"], 1)
                    Ct.wait("uh1")
                    Ct.free("uc2")
                    nc.vector.tensor_copy(u_h[:, 0, :], u[:, :]).then_inc(S["ul_ok"], 1)
                    Ct.wait("ul_ok")
                    nc.vector.tensor_tensor(u_l[:, :], u[:, :], u_h[:, 0, :], ALU.subtract).then_inc(S["uh2"], 1)
                    Ct.wait("uh2")
                    nc.vector.tensor_copy(u_h[:, 1, :], u_l[:, :]).then_inc(S["ull_ok"], 1)
                    Ct.wait("ull_ok")
                    nc.vector.tensor_tensor(u_h[:, 2, :], u_l[:, :], u_h[:, 1, :], ALU.subtract).then_inc(S["uh3"], 1)
                    Ct.free("w_pe3")
                    for n in range(2):
                        nc.vector.tensor_tensor(uc[:, n, :, :], hot_c[:, :, :],
                                                u_h[:, n:n + 1, :].to_broadcast([128, 2 * C, Q]), ALU.mult).then_inc(S[f"uc{n}"], 1)
                    nc.vector.tensor_tensor(
                        hot_r[:, :, :].rearrange("s r (a q) -> s a r q", q=16),
                        rc_sm[:, side, 0, :].rearrange("s (a q) -> s a q", q=16).unsqueeze(2).to_broadcast([128, 4, R, 16]),
                        col_iota[:, :, :].unsqueeze(1).to_broadcast([128, 4, R, 16]), ALU.is_equal).then_inc(S["hotr"], 1)
                if A:
                    av = bD[:, 0:8 * 2 * (HD + 1)].rearrange("q (h o d) -> q h o d", h=8, o=2)
                    A.wait("av_pe")
                    nc.vector.reciprocal(rsum[:, :, :, :], av[:, :, :, HD:HD + 1]).then_inc(S["rs_ok"], 1)
                    A.wait("rs_ok")
                    A.wait("xT_pe")
                    nc.vector.tensor_tensor(xn[:, :].rearrange("q (h o d) -> q h o d", h=8, o=2), av[:, :, :, 0:HD],
                                            rsum[:, :, :, :].to_broadcast([128, 8, 2, HD]), ALU.mult).then_inc(S["o_ok"], 1)
                if B:
                    B.wait_apart("best_v")
                    for h in range(RH):
                        last = nc.vector.max_index(besti[:, h, :], best[:, h, :], sums[:, h, :, :].rearrange("p a b -> p (a b)"))
                    last.then_inc(S["best_i"], 1)
                    B.free("ex_ok")
                    nc.vector.tensor_tensor(dif[:, :, :], best[:, :, :], best[:, :, 0:1].to_broadcast([128, RH, K8]),
                                            ALU.subtract).then_inc(S["dif_ok"], 1)
                    B.wait("best_i")
                    bi = besti[:, :, :].rearrange("p h k -> p (h k)")
                    nc.vector.tensor_scalar(ab_i[:, 0, :], bi, 3, None, ALU.logical_shift_right).then_inc(S["a_ok"], 1)
                    nc.vector.tensor_scalar(ab_i[:, 1, :], bi, 7, None, ALU.bitwise_and).then_inc(S["b_ok"], 1)
                    B.wait("a_ok")
                    B.wait("b_ok")
                    nc.vector.tensor_copy(ab_f[:, :, :], ab_i[:, :, :]).then_inc(S["ab_ok"], 1)
                if A:
                    A.wait("wo_pe")
                    A.free2("x1k_ok")
                    nc.vector.scalar_tensor_tensor(x1[:, side, :], bD[:, 0:DM], gates[:, 0:1], xt[:, side, :],
                                                   ALU.mult, ALU.add).then_inc(S["x1_ok"], 1)
                    A.wait("x1_ok")
                    nc.vector.bn_stats(st6b[:, :], x1[:, side, :]).then_inc(S["lstats"], 1)
                    A.wait_apart("lstats")
                    nc.vector.bn_aggr(mvb[:, :], st6b[:, :]).then_inc(S["lstats2"], 1)
                    A.wait("lstats2")
                    nc.vector.tensor_scalar(vepsb[:, :], mvb[:, 1:2], EPS, None, ALU.add).then_inc(S["leps_ok"], 1)
                if B:
                    B.wait("ab_ok")
                    nc.vector.tensor_tensor(eq[:, :, :, :], ab_f[:, :, :].unsqueeze(3).to_broadcast([128, 2, SLOTS, K8]),
                                            a_iota[:, :].unsqueeze(1).unsqueeze(1).to_broadcast([128, 2, SLOTS, K8]),
                                            ALU.is_equal).then_inc(S["eq_ok"], 1)
                    B.wait("eq_ok")
                    eq4 = eq[:, :, :, :].rearrange("p s (h k) a -> p (s h) k a", h=RH)
                    nc.vector.tensor_tensor(eq4, eq4, topf[:, :, :].unsqueeze(2).to_broadcast([128, 2 * RH, K8, K8]),
                                            ALU.mult).then_inc(S["pick_ok"], 1)
                    B.wait("pick_ok")
                    nc.vector.tensor_reduce(xy[:, :, :], eq[:, :, :, :], AX.X, ALU.add).then_inc(S["xy_ok"], 1)
                    B.wait("xy_ok")
                    nc.vector.scalar_tensor_tensor(e_i[:, :], xy[:, 0, :], float(NK), xy[:, 1, :], ALU.mult, ALU.add).then_inc(S["e_ok"], 1)
                    B.wait("e_ok")
                    nc.vector.tensor_scalar(rc_i[:, 0, :], e_i[:, :], R - 1, None, ALU.bitwise_and)
                    nc.vector.tensor_scalar(rc_i[:, 1, :], e_i[:, :], R.bit_length() - 1, None,
                                            ALU.logical_shift_right).then_inc(S["rci_ok"], 1)
                    B.wait("rci_ok")
                    if not isinstance(B.t, int) or B.t > 0:
                        dve.wait_ge(S["rows_out"], B.t * 32)
                    nc.vector.tensor_copy(r_h[:, :], rc_i[:, 0, :]).then_inc(S["rh_ok"], 1)
                    B.free("sm_pe")
                    nc.vector.tensor_copy(sm_in[:, 0, :, :], rc_i[:, 0:1, :].to_broadcast([128, 2, SLOTS]))
                    nc.vector.tensor_copy(sm_in[:, 1, 0, :], rc_i[:, 1, :])
                    nc.vector.tensor_scalar(sm_in[:, 1, 1, :], rc_i[:, 1, :], float(C), None, ALU.add).then_inc(S["rdup_ok"], 1)
                    B.wait("ex_ok")
                    nc.vector.reduce_sum(exs[:, :, 0], ex[:, :, :], AX.X).then_inc(S["exs_ok"], 1)
                    B.wait("exs_ok")
                    nc.vector.reciprocal(exr[:, :, :], exs[:, :, :]).then_inc(S["exr_ok"], 1)
                    B.wait("exr_ok")
                    for half in range(2):
                        last = nc.vector.tensor_tensor(sm_in[:, 2, half, :].rearrange("p (h k) -> p h k", h=RH), ex[:, :, :],
                                                       exr[:, :, :].to_broadcast([128, RH, K8]), ALU.mult)
                    last.then_inc(S["p_ok"], 1)
                if A:
                    A.wait("lrstd_ok")
                    A.wait("oT_pe")
                    nc.vector.tensor_scalar(xn[:, :], x1[:, side, :], mvb[:, 0:1], rstdb[:, 0:1],
                                            ALU.subtract, ALU.mult).then_inc(S["xn2_ok"], 1)
                    for n in range(2):
                        A.wait(f"tanh{n}")
                        A.free("hid_pe")
                        ch = slice(4 * n, 4 * n + 4)
                        nc.vector.scalar_tensor_tensor(up_act[:, ch, :], up_t[:, ch, :], 1.0, up_pre[:, ch, :],
                                                       ALU.add, ALU.mult).then_inc(S[f"act{n}"], 1)
                if Ct:
                    Ct.wait("out_pe")
                    Ct.wait("x1k_ok")
                    nc.vector.scalar_tensor_tensor(x1k[:, side, :], bG0[:, 0:DM], gates[:, 1:2], x1k[:, side, :],
                                                   ALU.mult, ALU.add).then_inc(S["y_ok"], 1)
                if B:
                    B.wait("sm_pe")
                    B.free2("hotr")
                    B.free2("hotc")
                    for half in range(2):
                        rows, cols = slice(half * 64, half * 64 + 64), slice(half * Q, half * Q + Q)
                        src = bG1[rows, 0:384].rearrange("p (n t) -> p n t", n=3)
                        last = nc.vector.tensor_copy(rc_sm[rows, b, :, :], src[:, 0:2, cols])
                        last2 = nc.vector.tensor_copy(p_sm[rows, b, :], src[:, 2, cols])
                    last.then_inc(S["sm_rc"], 1)
                    last2.then_inc(S["sm_p"], 1)

            pipeline(dve, turn)

        @block.tensor
        def _(pe):
            mm = nc.tensor.matmul
            pe.wait_ge(S["consts"], 1)
            groups = list(weight_groups())
            for n, (arrived, srcs, dst, scale) in enumerate(groups):
                pe.wait_ge(S[arrived], 16)
                if n >= 8:
                    pe.wait_ge(S["wT_dve"], n - 7)
                for j, s in enumerate(srcs):
                    rows = s.shape[0]
                    last = nc.tensor.transpose(banks[n % 8][0:s.shape[1], 128 * j:128 * j + rows], s, ident[0:rows, 0:rows])
                last.then_inc(S["wT_pe"], 1)
            pe.wait_ge(S["wT_dve"], len(groups))
            pe.wait_ge(S["wr_in"], 32)
            for s in range(2):
                rows = slice(64 * s, 64 * s + 64)
                for h in range(RH):
                    last = mm(banks[s][:, NK * h:NK * h + NK], wr_n[rows, h, :], keysT[rows, h, :], start=True, stop=True)
            last.then_inc(S["simw_pe"], 1)
            pe.wait_ge(S["simw_done"], 1)
            pe.wait_ge(S["ue_in"], 16)

            def turn(A, B, Ct, side):
                b = 1 - side

                def gather(k):
                    Ct.wait("hotrT")
                    Ct.wait("z_sb3")
                    Ct.wait("zll_ok")
                    if k == 0:
                        Ct.free("y_ok")
                    elif k == 1:
                        Ct.wait("sm_p")
                        Ct.wait("sm_rc")
                    else:
                        Ct.wait(f"gm{k - 2}")
                    parts = [zz[:, side, :, :].bitcast(H)[:, :, 1::2] for zz in (z, zl)] + [zll[:, side, :, :]]
                    for q in range(16 * k, 16 * k + 16):
                        for n, part in enumerate(parts):
                            last = mm(bG[k % 2][:, 32 * (q - 16 * k):32 * (q - 16 * k) + 32], hot_rT[:, q, :],
                                      part.rearrange("r c (h q) -> r h c q", h=2)[:, :, :, q], start=(n == 0), stop=(n == 2))
                    last.then_inc(S[f"g_pe{k}"], 1)

                def scatter(k):
                    if k == 0:
                        Ct.wait("hotr")
                        for n in range(3):
                            Ct.wait(f"uc{n}")
                    Ct.wait(f"gm{k + 2}" if k < 2 else f"w_sb{k - 2}")
                    for q in range(16 * k, 16 * k + 16):
                        for n in range(3):
                            last = mm(bG[k % 2][:, 32 * (q - 16 * k):32 * (q - 16 * k) + 32], hot_r[:, :, q], uc[:, n, :, q],
                                      start=(n == 0), stop=(n == 2))
                    last.then_inc(S[f"w_pe{k}"], 1)

                if A:
                    A.wait("xn_ok")
                    A.wait_dma_side(f"ctx_in{side}")
                    A.free("x2T_sb")
                    for k in range(2):
                        nc.tensor.transpose(bT[:, 128 * k:128 * k + 128], xn[:, 128 * k:128 * k + 128], ident[:, :])
                    nc.tensor.transpose(bT[0:CTX, 256:384], ct[:, side, :], ident[:, :]).then_inc(S["xT_pe"], 1)
                if Ct:
                    gather(0)
                if A:
                    A.wait("xT_sb")
                    A.wait("ctxT_sb")
                    A.free("hid_sb")
                    for m in range(2):
                        for k in range(2):
                            mm(bD[:, 128 * m:128 * m + 128], WqT[:, k, 128 * m:128 * m + 128], xnT[:, k, :], start=(k == 0), stop=(k == 1))
                    for m in range(2):
                        last = mm(bD[:, 256 + 128 * m:384 + 128 * m], WkvT[:, 128 * m:128 * m + 128], ctxT[:, :, 0, :], start=True, stop=True)
                    last.then_inc(S["q_pe"], 1)
                    A.free("sim_sb0")
                    for s in range(2):
                        last = mm(bP0[:, 256 * s:256 * s + 256], ctxT[:, s, :, :].rearrange("l d k -> l (d k)"), WkvT[:, DM:2 * DM],
                                  start=True, stop=True)
                    last.then_inc(S["v_pe"], 1)
                if Ct:
                    gather(1)
                if A:
                    A.wait("q_sb")
                    for half in range(2):
                        A.free(f"z_sb{2 + half}")
                        mm(bS[half][:, :], ident_h[:, :], causal[:, :, :].rearrange("p h k -> p (h k)"), start=True, stop=False)
                        A.wait(f"kdiag{half}")
                        for s in range(2):
                            last = mm(bS[half][64 * s:64 * s + 64, :], qT[:, half, 64 * s:64 * s + 64],
                                      k_diag[:, half, s, :, :].rearrange("p h k -> p (h k)"), start=False, stop=True)
                        last.then_inc(S[f"s_pe{half}"], 1)
                if Ct:
                    gather(2)
                    gather(3)
                if A:
                    for n in range(2):
                        A.wait(f"exp{n}")
                        if n == 0:
                            A.wait("v_sb0")
                            A.wait("v_sb1")
                        else:
                            A.free("sim_sb1")
                        for j in range(4):
                            hp = 4 * n + j
                            last = nc.tensor.transpose(bP[n][:, 128 * j:128 * j + 128],
                                                       P[:, 2 * hp:2 * hp + 2, :].rearrange("p h k -> p (h k)"), ident[:, :])
                        last.then_inc(S[f"pt_pe{n}"], 1)
                    A.wait("pt_sb0")
                    A.wait("pt_sb1")
                    A.wait("k_sb")
                    for s in range(2):
                        for hp in range(8):
                            last = mm(bD[64 * s:64 * s + 64, 34 * hp:34 * hp + 34], PT[:, hp, 64 * s:64 * s + 64],
                                      v_diag[:, s, hp, :, :].rearrange("p o d -> p (o d)"), start=True, stop=True)
                    last.then_inc(S["av_pe"], 1)
                if Ct:
                    scatter(0)
                if A:
                    A.wait("o_ok")
                    for k in range(2):
                        last = nc.tensor.transpose(bT[:, 128 * k:128 * k + 128], xn[:, 128 * k:128 * k + 128], ident[:, :])
                    last.then_inc(S["oT_pe"], 1)
                if Ct:
                    scatter(1)
                if A:
                    A.wait("oT_sb")
                    for k in range(2):
                        last = mm(bD[:, 0:DM], oT[:, k, :], WoT[:, k, :], start=(k == 0), stop=(k == 1))
                    last.then_inc(S["wo_pe"], 1)
                if Ct:
                    scatter(2)
                if A:
                    A.wait("xn2_ok")
                    for k in range(2):
                        last = nc.tensor.transpose(bT[:, 128 * k:128 * k + 128], xn[:, 128 * k:128 * k + 128], ident[:, :])
                    last.then_inc(S["x2T_pe"], 1)
                if Ct:
                    scatter(3)
                if A:
                    A.wait("x2T_sb")
                    for n in range(2):
                        A.wait(f"sub{n}")
                        for m in range(4):
                            c = 4 * n + m
                            for k in range(2):
                                last = mm(bS[n][:, 128 * m:128 * m + 128], WupT[:, k, 128 * c:128 * c + 128], xn2T[:, k, :],
                                          start=(k == 0), stop=(k == 1))
                        last.then_inc(S[f"up_pe{n}"], 1)
                if Ct:
                    Ct.wait("w_sb3")
                    for c in range(C):
                        last = mm(bG0[:, 0:DM], coef[:, c, :, :].rearrange("r h q -> r (h q)"), ue[:, c, :], start=(c == 0), stop=(c == C - 1))
                    last.then_inc(S["out_pe"], 1)
                if A:
                    for c in range(DUP // 128):
                        if c % 4 == 0:
                            A.wait(f"act{c // 4}")
                        last = mm(bD[:, 0:TILE], WdT[:, c, :], up_act[:, c, :], start=(c == 0), stop=(c == DUP // 128 - 1))
                    last.then_inc(S["hid_pe"], 1)
                if B:
                    if Ct:
                        Ct.wait("w_sb3")
                    B.wait("rdup_ok")
                    B.wait("p_ok")
                    for n in range(3):
                        last = nc.tensor.transpose(bG1[:, 128 * n:128 * n + 128], sm_in[:, n, :, :].rearrange("p a s -> p (a s)"), ident[:, :])
                    last.then_inc(S["sm_pe"], 1)
                if A:
                    A.wait("hid_sb")
                    for s in range(2):
                        last = mm(bP[s][:, 0:RH * NK], hT[:, :], simW[:, s, :], start=True, stop=True)
                        last.then_inc(S[f"sim_pe{s}"], 1)
                    for n in range(4):
                        if n >= 2:
                            A.wait(f"z_sb{n - 2}")
                        for m in range(4):
                            c = 4 * n + m
                            last = mm(bS[n % 2][:, 128 * m:128 * m + 128], deT[:, R * c:R * c + R], hT[:, :], start=True, stop=True)
                        last.then_inc(S[f"z_pe{n}"], 1)

            pipeline(pe, turn)


_INS = ["x", "ctx_512", "g_xattn", "g_ffn", "L0_xattn_Wq", "L0_xattn_Wkv_expand", "L0_xattn_Wout", "L0_ffn_W_up",
        "L0_ffn_b_up", "L0_ffn_W_down", "L0_ffn_b_down", "L0_ffn_W_q", "L0_ffn_keys", "L0_ffn_down_embed",
        "L0_ffn_up_embed"]


def kernel(**inputs):
    import numpy as _np
    import concourse.bacc as _bacc
    from concourse import mybir as _mybir
    from concourse.bass_utils import run_bass_kernel_spmd as _run

    nc = _bacc.Bacc("TRN2", target_bir_lowering=False, num_devices=1)
    arrays, args = {}, []
    for name in _INS:
        a = _np.ascontiguousarray(inputs[name])
        arrays[f"in_{name}"] = a
        args.append(nc.dram_tensor(f"in_{name}", a.shape, _mybir.dt.from_np(a.dtype), kind="ExternalInput").ap())
    args.append(nc.dram_tensor("out", (64, 64, 256), _mybir.dt.float32, kind="ExternalOutput").ap())
    flamingo_layer(nc, *args)
    r = _run(nc, [arrays], core_ids=[0])
    return r.results[0]["out"]
```

```python
import concourse.bass as bass
from concourse import mybir
from contextlib import ExitStack

TOKENS, DM, CTX = 4096, 256, 64
SEQ, HEADS, HD = 64, 16, 16
DUP, DP = 1024, 128
RH, NK, K8 = 8, 45, 8
SLOTS = RH * K8
NE, R = 2048, 128
C = NE // R
TILE = 128
TILES = TOKENS // TILE
Q = TILE // 2
EPS = 1e-5
MASKED = -1e30


def flamingo_layer(nc, x, ctx_512, g_xattn, g_ffn, Wq, Wkv, Wout, W_up, b_up, W_down, b_down, W_r,
                   keys, down_embed, up_embed, out):
    F, H, U = mybir.dt.float32, mybir.dt.bfloat16, mybir.dt.uint32
    ALU, ACT, AX = mybir.AluOpType, mybir.ActivationFunctionType, mybir.AxisListType

    x_d = x.rearrange("b s d -> (b s) d").rearrange("(t p) d -> t p d", p=TILE)
    ctx_d = ctx_512.rearrange("b s d -> (b s) d").rearrange("(t p) d -> t p d", p=TILE)
    out_d = out.rearrange("b s d -> (b s) d").rearrange("(t p) d -> t p d", p=TILE)
    rows_d = nc.dram_tensor("expert_rows", (2, Q, 2, SLOTS), H, kind="Internal").ap()

    es = ExitStack()
    with es:
        def sb(name, shape, dt=F):
            return es.enter_context(nc.sbuf_tensor(name, shape, dt))

        def sem(name):
            return es.enter_context(nc.semaphore(name))

        ident = sb("ident", [128, 128])
        ident_h = sb("ident_h", [128, 128], H)
        causal = sb("causal", [128, 8, SEQ], H)
        head_of = sb("head_of", [128, 8])
        col_iota = sb("col_iota", [128, R, 16], H)
        a_iota = sb("a_iota", [128, K8, 2 * SLOTS], H)
        p_iota = sb("p_iota", [128, 1])
        minus_half = sb("minus_half", [128, 1])
        gates = sb("gates", [128, 2])
        bup_sb = sb("bup_sb", [128, DUP // 128])
        bdn_sb = sb("bdn_sb", [128, 1])
        WqT = sb("WqT", [128, 2, DM])
        WkvT = sb("WkvT", [CTX, 2 * DM])
        WoT = sb("WoT", [128, 2, DM])
        WupT = sb("WupT", [128, 2, DUP])
        WdT = sb("WdT", [128, DUP // 128, DP])
        simW = sb("simW", [DP, 2, RH * NK])
        deT = sb("deT", [DP, NE])
        ue = sb("ue", [R, C, DM])

        xt = sb("xt", [128, 2, DM])
        ct = sb("ct", [128, 2, CTX])
        st6 = sb("st6", [128, 6])
        mv = sb("mv", [128, 2])
        veps = sb("veps", [128, 1])
        rstd = sb("rstd", [128, 1])
        st6b = sb("st6b", [128, 6])
        mvb = sb("mvb", [128, 2])
        vepsb = sb("vepsb", [128, 1])
        rstdb = sb("rstdb", [128, 1])
        xn1 = sb("xn1", [128, DM])
        xn = sb("xn", [128, DM])
        xnT = sb("xnT", [128, 2, TILE])
        ctxT = sb("ctxT", [CTX, 2, 2, SEQ])
        qT = sb("qT", [128, 2, TILE])
        kT = sb("kT", [128, 2, TILE])
        k_diag = sb("k_diag", [128, 2, 2, 8, SEQ])
        v_diag = sb("v_diag", [128, 2, 8, 2, HD + 1])
        smax = sb("smax", [128, HEADS])
        nbias = sb("nbias", [128, HEADS])
        P = sb("P", [128, HEADS, SEQ])
        PT = sb("PT", [128, 8, TILE])
        rsum = sb("rsum", [128, 8, 2, 1])
        oT = sb("oT", [128, 2, TILE])
        x1 = sb("x1", [128, 2, DM])
        xn2T = sb("xn2T", [128, 2, TILE])
        up_pre = P[:, :, :].rearrange("p h k -> p (h k)").rearrange("p (a t) -> p a t", a=8)
        up_t = PT
        up_act = PT
        hT = sb("hT", [DP, TILE])
        sims = sb("sims", [128, 2, 2 * RH, NK])
        z = sb("z", [R, 2, C, TILE])
        zl = sb("zl", [R, 2, C, TILE])
        zll = sb("zll", [R, 2, C, TILE], H)

        x1k = sb("x1k", [128, 2, DM])
        top = sb("top", [128, 2 * RH, K8])
        topi = sb("topi", [128, 2 * RH, K8], U)
        top_rep = sb("top_rep", [128, K8, 2 * RH, K8], H)
        sums = sb("sums", [128, RH, K8, K8])
        best = sb("best", [128, RH, K8])
        besti = sb("besti", [128, RH, K8], U)
        ab_i = sb("ab_i", [128, 2, SLOTS], U)
        ab_h = sb("ab_h", [128, 2 * SLOTS], H)
        eq = sb("eq", [128, K8, 2 * SLOTS], H)
        xy = sb("xy", [128, 2, SLOTS])
        e_i = sb("e_i", [128, SLOTS], U)
        rc_i = sb("rc_i", [128, 2, SLOTS], U)
        r_h = sb("r_h", [128, SLOTS], H)
        sm_in = sb("sm_in", [128, 3, 2, SLOTS])
        dif = sb("dif", [128, RH, K8])
        ex = sb("ex", [128, RH, K8])
        exs = sb("exs", [128, RH, 1])
        exr = sb("exr", [128, RH, 1])
        rc_sm = sb("rc_sm", [128, 2, 2, Q], H)
        p_sm = sb("p_sm", [128, 2, Q])

        hot_rT = sb("hot_rT", [R, Q, 2 * SLOTS], H)
        hot_r = sb("hot_r", [128, R, Q], H)
        hot_c = sb("hot_c", [128, 2 * C, Q], H)
        picked = sb("picked", [128, 2, 16, 2 * C])
        zs = sb("zs", [128, Q])
        zp = sb("zp", [128, Q])
        zt = sb("zt", [128, Q])
        u = sb("u", [128, Q])
        u_l = sb("u_l", [128, Q])
        u_h = sb("u_h", [128, 3, Q], H)
        uc = sb("uc", [128, 3, 2 * C, Q], H)
        coef = sb("coef", [R, C, 2, Q])

        banks = [es.enter_context(nc.psum_tensor(f"bank{i}", [128, 512], F)) for i in range(8)]
        bT, bD, bG0, bG1, bS0, bS1, bP0, bP1 = banks
        bG, bS, bP = (bG0, bG1), (bS0, bS1), (bP0, bP1)

        wq_n = P[:, 0:8, :].rearrange("p h k -> p (h k)").rearrange("p (a k) -> p a k", a=2)
        wo_n = P[:, 8:16, :].rearrange("p h k -> p (h k)").rearrange("p (a k) -> p a k", a=2)
        wkv_n = PT[:, 0:2, :].rearrange("p a b -> p (a b)").rearrange("p (a k) -> p a k", a=4)
        wup_n = z[:, 0, :, :].rearrange("p c t -> p (c t)").rearrange("p (a k) -> p a k", a=8)
        wdn_n = z[:, 1, 0:8, :].rearrange("p a t -> p (a t)")
        wr_n = zl[:, 1, 0:8, :]
        keys_n = zl[:, 1, 8:16, :]
        de_n = zl[:, 0, :, :]
        keysT = z[:, 1, 8:16, 0:NK]

        S = {n: sem(n) for n in (
            "wq_in wkvo_in wup_in wdn_in router_in de_in ue_in small_in "
            "const_step ident_ok consts gate_done wT_pe wT_dve wT_act simw_pe simw_done "
            "x_in0 x_in1 ctx_in0 ctx_in1 stats stats2 eps_ok rstd_ok xn_ok xT_pe xT_sb ctxT_sb q_pe v_pe q_sb k_sb v_sb0 v_sb1 "
            "kdiag0 kdiag1 s_pe0 s_pe1 max0 max1 nb0 nb1 exp0 exp1 pt_pe0 pt_pe1 pt_sb0 pt_sb1 av_pe rs_ok o_ok "
            "oT_pe oT_sb wo_pe x1_ok lstats lstats2 leps_ok lrstd_ok xn2_ok x2T_pe x2T_sb "
            "up_pe0 up_pe1 pre0 pre1 tanh0 tanh1 act0 act1 hid_pe hid_sb sim_pe0 sim_pe1 sim_sb0 sim_sb1 "
            "z_pe0 z_pe1 z_pe2 z_pe3 z_sb0 z_sb1 z_sb2 z_sb3 "
            "zl_ok zll_ok x1k_ok top_v top_i rep_ok sums_ok best_v best_i b_ok ab_ok eq_ok pick_ok tree4 tree2 xy_ok "
            "e_ok rci_ok rh_ok rdup_ok dif_ok ex_ok exs_ok exr_ok p_ok sm_pe sm_ok rows_out "
            "rows_in0 rows_in1 hotrT0 hotrT1 hotr0 hotr1 hotr2 hotr3 hotc g_pe0 g_pe1 g_pe2 g_pe3 gm0 gm1 gm2 gm3 zs0 zs1 zs2 zs3 zp_ok zt_ok u_ok uh1 uh2 uh3 ul_ok "
            "uc0 uc1 uc2 w_pe0 w_pe1 w_pe2 w_pe3 w_sb0 w_sb1 w_sb2 w_sb3 out_pe y_ok y_out0 y_out1 settled"
        ).split()}

        class Tile:

            def __init__(self, eng, t, count, pair):
                self.eng, self.t, self.pair, self.count = eng, t, pair, count
                self.later = not isinstance(t, int)

            def wait(self, name):
                self.eng.wait_ge(S[name], self.count(1))

            def wait_apart(self, name):
                self.wait(name)
                self.eng.sem_inc(S["settled"], 1)

            def wait_dma(self, name, n=1):
                self.eng.wait_ge(S[name], 16 * n * self.count(1))

            def wait_dma_side(self, name):
                self.eng.wait_ge(S[name], 16 * (self.pair + 1))

            def free(self, name, n=1):
                if self.later or self.t > 0:
                    self.eng.wait_ge(S[name], n * self.count(0))

            def free2(self, name, apart=False):
                if self.later or self.t > 1:
                    self.eng.wait_ge(S[name], self.count(-1))
                    if apart:
                        self.eng.sem_inc(S["settled"], 1)

            def free_dma_side(self, name):
                if self.later or self.pair > 0:
                    self.eng.wait_ge(S[name], 16 * self.pair)

        DEPTH = 5

        def one_turn(eng, turn, i):
            tiles = [Tile(eng, i - d, lambda k, t=i - d: t + k, (i - d) // 2) if 0 <= i - d < TILES else None
                     for d in range(DEPTH)]
            turn(*tiles, (i - 1) % 2)

        def start(eng, turn, i):
            one_turn(eng, turn, i)

        def pipeline(eng, turn):

            def at(i):
                one_turn(eng, turn, i)

            first = DEPTH + 1
            for i in range(2, first):
                at(i)
            with eng.Fori(0, (TILES - first) // 2) as n:
                base = [eng.snap(n * 2 + k) for k in range(first + 3)]
                for i in range(first, first + 2):
                    tiles = [Tile(eng, base[i - d], lambda k, t=i - d: base[t + k], n + (i - d) // 2) for d in range(DEPTH)]
                    turn(*tiles, (i - 1) % 2)
            for i in range(TILES, TILES + DEPTH - 1):
                at(i)

        def top_half(ap):
            return ap.bitcast(H)[:, :, 1::2]

        def weight_groups():
            yield "wq_in", 1, [wq_n[:, o, k * 128:k * 128 + 128] for k in range(2) for o in range(2)], \
                WqT[:, :, :].rearrange("p k (o m) -> p (k o) m", o=2), 1.0
            yield "wkvo_in", 2, [wkv_n[:, o, :] for o in range(4)], WkvT[:, :].rearrange("p (o m) -> p o m", o=4), 1.0
            yield "wkvo_in", 2, [wo_n[:, o, k * 128:k * 128 + 128] for k in range(2) for o in range(2)], \
                WoT[:, :, :].rearrange("p k (o m) -> p (k o) m", o=2), 1.0
            for k in range(2):
                for g in range(2):
                    yield "wup_in", 1, [wup_n[:, 4 * g + o, k * 128:k * 128 + 128] for o in range(4)], \
                        WupT[:, k, 512 * g:512 * g + 512].rearrange("p (o m) -> p o m", o=4), 1.0
            for g in range(2):
                yield "wdn_in", 1, [wdn_n[:, 128 * (4 * g + o):128 * (4 * g + o) + 128] for o in range(4)], \
                    WdT[:, 4 * g:4 * g + 4, :], 0.5
            for g in range(4):
                yield "de_in", 1, [de_n[:, 4 * g + o, :] for o in range(4)], \
                    deT[:, 512 * g:512 * g + 512].rearrange("p (o m) -> p o m", o=4), 1.0
            for g in range(2):
                yield "router_in", 3, [keys_n[0:NK, 4 * g + o, :] for o in range(4)], keysT[:, 4 * g:4 * g + 4, :], 1.0

        ATTENTION, OTHERS = range(0, 3), range(3, len(list(weight_groups())))

        def move_weights(eng, odd, numbers):
            for n, (_, _, srcs, dst, scale) in enumerate(weight_groups()):
                if n % 2 != odd or n not in numbers:
                    continue
                eng.wait_ge(S["wT_pe"], n + 1)
                rows, w = srcs[0].shape[1], srcs[0].shape[0]
                src = banks[n % 8][0:rows, :].rearrange("p (a w) -> p a w", w=128)[:, 0:len(srcs), 0:w]
                if odd:
                    nc.scalar.activation(dst, src, ACT.Copy, scale=scale).then_inc(S["wT_act"], 1)
                elif scale == 1.0:
                    nc.vector.tensor_copy(dst, src).then_inc(S["wT_dve"], 1)
                else:
                    nc.vector.tensor_scalar(dst, src, scale, None, ALU.mult).then_inc(S["wT_dve"], 1)

        block = es.enter_context(nc.Block())

        @block.sync
        def _(sp):
            def turn(L, A, Fw, B, Ct, side):
                if L:
                    ls = 1 - side
                    L.free2("x1_ok", apart=True)
                    sp.dma_start(xt[:, ls, :], x_d[bass.ds(L.t, 1), :, :].rearrange("a p d -> p (a d)")).then_inc(S[f"x_in{ls}"], 16)
                    L.free2("xT_pe", apart=True)
                    sp.dma_start(ct[:, ls, :], ctx_d[bass.ds(L.t, 1), :, :].rearrange("a p d -> p (a d)")).then_inc(S[f"ctx_in{ls}"], 16)
                if B:
                    B.wait_apart("rh_ok")
                    for half in range(2):
                        sp.dma_start(rows_d[side, :, half, :], r_h[half * Q:half * Q + Q, :]).then_inc(S["rows_out"], 16)
                    B.wait_dma("rows_out", 2)
                    sp.sem_inc(S["settled"], 1)
                    B.free("g_pe3")
                    for part in range(2):
                        qs = slice(part * Q // 2, (part + 1) * Q // 2)
                        sp.dma_start(hot_rT[:, qs, :].rearrange("r q s -> r (q s)"),
                                     rows_d[side:side + 1, qs, :, :].rearrange("b q h s -> b (q h s)").to_broadcast([128, Q * SLOTS]),
                                     ).then_inc(S[f"rows_in{part}"], 16)
                if Ct:
                    Ct.wait_apart("y_ok")
                    sp.dma_start(out_d[bass.ds(Ct.t, 1), :, :].rearrange("a p d -> p (a d)"), x1k[:, 1 - side, :])\
                        .then_inc(S[f"y_out{1 - side}"], 16)

            sp.dma_start(wq_n, Wq.rearrange("(a p) k -> p a k", p=128)).then_inc(S["wq_in"], 16)
            start(sp, turn, 0)
            sp.dma_start(wkv_n, Wkv.rearrange("(a p) k -> p a k", p=128)).then_inc(S["wkvo_in"], 16)
            sp.dma_start(bup_sb[:, :], b_up.rearrange("(a p) -> p a", p=128), allow_slow_non_contiguous=True).then_inc(S["small_in"], 16)
            sp.dma_start(bdn_sb[:, :], b_down.rearrange("(p a) -> p a", a=1)).then_inc(S["small_in"], 16)
            sp.dma_start(gates[:, 0:1], g_xattn.rearrange("(a b) -> a b", b=1).to_broadcast([128, 1])).then_inc(S["small_in"], 16)
            sp.dma_start(gates[:, 1:2], g_ffn.rearrange("(a b) -> a b", b=1).to_broadcast([128, 1])).then_inc(S["small_in"], 16)
            sp.dma_start(wo_n, Wout.rearrange("(a p) k -> p a k", p=128)).then_inc(S["wkvo_in"], 16)
            start(sp, turn, 1)
            for s in range(2):
                sp.dma_start(wr_n[s * 64:s * 64 + 64, :, :],
                             W_r[s * 512:s * 512 + 512, :].rearrange("(h n) p -> n h p", n=64)).then_inc(S["router_in"], 16)
            sp.dma_start(wup_n, W_up.rearrange("(a p) k -> p a k", p=128)).then_inc(S["wup_in"], 16)
            sp.dma_start(wdn_n, W_down).then_inc(S["wdn_in"], 16)
            sp.dma_start(keys_n[0:NK, :, :].rearrange("k h (s n) -> k h s n", s=2),
                         keys.rearrange("h k s n -> k h s n")).then_inc(S["router_in"], 16)
            sp.dma_start(de_n, down_embed.rearrange("(c r) d -> r c d", r=R)).then_inc(S["de_in"], 16)
            sp.dma_start(ue[:, :, :], up_embed.rearrange("(c r) d -> r c d", r=R)).then_inc(S["ue_in"], 16)
            pipeline(sp, turn)
            for side in range(2):
                sp.wait_ge(S[f"y_out{side}"], 16 * (TILES // 2))

        @block.gpsimd
        def _(pool):
            def turn(L, A, Fw, B, Ct, side):
                def k_blocks(half):
                    A.wait("k_sb")
                    A.free(f"s_pe{half}")
                    nc.gpsimd.tensor_tensor(
                        k_diag[:, half, :, :, :],
                        kT[:, half, :].rearrange("p (b k) -> p b k", b=2).unsqueeze(2).to_broadcast([128, 2, 8, SEQ]),
                        head_of[:, :].unsqueeze(1).unsqueeze(3).to_broadcast([128, 2, 8, SEQ]),
                        ALU.mult).then_inc(S[f"kdiag{half}"], 1)

                if A:
                    k_blocks(0)
                    k_blocks(1)
                if B:
                    B.wait("z_sb3")
                    B.free2("g_pe3")
                    nc.gpsimd.tensor_tensor(zl[:, side, :, :], z[:, side, :, :], top_half(z[:, side, :, :]), ALU.subtract).then_inc(S["zl_ok"], 1)
                if A:
                    A.wait("leps_ok")
                    nc.gpsimd.tensor_tensor(rstdb[:, :], vepsb[:, :], minus_half[:, :], ALU.pow).then_inc(S["lrstd_ok"], 1)
                if L:
                    L.wait("eps_ok")
                    nc.gpsimd.tensor_tensor(rstd[:, :], veps[:, :], minus_half[:, :], ALU.pow).then_inc(S["rstd_ok"], 1)
                if B:
                    B.wait("zl_ok")
                    nc.gpsimd.tensor_tensor(zll[:, side, :, :], zl[:, side, :, :], top_half(zl[:, side, :, :]), ALU.subtract).then_inc(S["zll_ok"], 1)

            steps = [0]

            def step(ins):
                ins.then_inc(S["const_step"], 1)
                steps[0] += 1
                pool.wait_ge(S["const_step"], steps[0])

            small = dict(allow_small_or_imprecise_dtypes=True)
            step(nc.gpsimd.memset(ident[:, :], 0.0))
            step(nc.gpsimd.memset(minus_half[:, :], -0.5))
            nc.gpsimd.affine_select(out=ident[:, :], in_=ident[:, :], compare_op=ALU.not_equal, fill=1.0,
                                    base=0, pattern=[[-1, 128]], channel_multiplier=1).then_inc(S["ident_ok"], 1)
            start(pool, turn, 0)
            step(nc.gpsimd.memset(causal[:, :, :], 0.0))
            step(nc.gpsimd.memset(head_of[:, :], 1.0))
            step(nc.gpsimd.memset(v_diag[:, :, :, :, :], 0.0))
            for s in range(2):
                rows = causal[s * SEQ:s * SEQ + SEQ, :, :]
                step(nc.gpsimd.affine_select(out=rows, in_=rows, compare_op=ALU.is_ge, fill=MASKED,
                                             base=0, pattern=[[0, 8], [-1, SEQ]], channel_multiplier=1))
            for odd in range(2):
                step(nc.gpsimd.memset(v_diag[odd * 64:odd * 64 + 64, :, :, odd, HD:HD + 1], 1.0))
            step(nc.gpsimd.affine_select(out=head_of[:, :], in_=head_of[:, :], compare_op=ALU.is_ge, fill=0.0,
                                         base=0, pattern=[[-HD, 8]], channel_multiplier=1))
            step(nc.gpsimd.affine_select(out=head_of[:, :], in_=head_of[:, :], compare_op=ALU.is_ge, fill=0.0,
                                         base=HD - 1, pattern=[[HD, 8]], channel_multiplier=-1))
            pool.wait_ge(S["ident_ok"], 1)
            nc.gpsimd.tensor_copy(ident_h[:, :], ident[:, :]).then_inc(S["consts"], 1)
            start(pool, turn, 1)
            step(nc.gpsimd.iota(col_iota[:, :, :], pattern=[[1, R], [0, 16]], base=0, channel_multiplier=0, **small))
            step(nc.gpsimd.iota(a_iota[:, :, :], pattern=[[1, K8], [0, 2 * SLOTS]], base=0, channel_multiplier=0, **small))
            nc.gpsimd.iota(p_iota[:, :], pattern=[[0, 1]], base=0, channel_multiplier=1, **small).then_inc(S["consts"], 1)
            pool.wait_ge(S["simw_done"], 1)
            pipeline(pool, turn)

        @block.scalar
        def _(act):
            def turn(L, A, Fw, B, Ct, side):
                def copy(dst, src, done, scale=1.0):
                    nc.scalar.activation(dst, src, ACT.Copy, scale=scale).then_inc(S[done], 1)

                def up_bias(n):
                    Fw.wait(f"up_pe{n}")
                    Fw.wait("pt_pe1")
                    Fw.wait("av_pe")
                    for m in range(4):
                        c = 4 * n + m
                        last = nc.scalar.activation(up_pre[:, c, :], bS[n][:, 128 * m:128 * m + 128], ACT.Identity,
                                                    bias=bup_sb[:, c:c + 1])
                    last.then_inc(S[f"pre{n}"], 1)

                def up_tanh(n):
                    Fw.wait(f"pre{n}")
                    nc.scalar.activation(up_t[:, 4 * n:4 * n + 4, :], up_pre[:, 4 * n:4 * n + 4, :], ACT.Tanh,
                                         scale=0.5).then_inc(S[f"tanh{n}"], 1)

                def values(odd):
                    rows = slice(odd * 64, odd * 64 + 64)
                    A.wait("v_pe")
                    A.free("av_pe")
                    copy(v_diag[rows, :, :, odd, 0:HD],
                         bP0[rows, :].rearrange("k (b h o d) -> k b h o d", b=2, h=8, o=2)[:, :, :, odd, :], f"v_sb{odd}")

                def similarities(s):
                    Fw.free2("top_i")
                    Fw.wait(f"sim_pe{s}")
                    copy(sims[:, 1 - side, RH * s:RH * s + RH, :], bP[s][:, 0:RH * NK].rearrange("t (h k) -> t h k", h=RH), f"sim_sb{s}")

                def exps(half):
                    A.wait(f"nb{half}")
                    if Fw:
                        Fw.wait("act1")
                    for h in range(8 * half, 8 * half + 8):
                        last = nc.scalar.activation(P[:, h, :], bS[half][:, SEQ * (h % 8):SEQ * (h % 8) + SEQ], ACT.Exp,
                                                    bias=nbias[:, h:h + 1], scale=HD ** -0.5)
                    last.then_inc(S[f"exp{half}"], 1)

                def probs_T(n):
                    A.wait(f"pt_pe{n}")
                    if Fw:
                        Fw.wait("hid_pe")
                    copy(PT[:, 4 * n:4 * n + 4, :], bP[n][:, :].rearrange("p (a t) -> p a t", a=4), f"pt_sb{n}")

                def coef_copy(k):
                    Ct.wait(f"w_pe{k}")
                    if k == 0:
                        Ct.free("out_pe")
                    copy(coef[:, :, :, 16 * k:16 * k + 16].rearrange("r c h q -> r q h c"),
                         bG[k % 2][:, :].rearrange("r (q h c) -> r q h c", q=16, h=2), f"w_sb{k}")

                def z_copy(n):
                    if n == 0:
                        Fw.free2("g_pe3")
                        Fw.free2("zll_ok")
                    Fw.wait(f"z_pe{n}")
                    copy(z[:, 1 - side, 4 * n:4 * n + 4, :], bS[n % 2][:, :].rearrange("r (c t) -> r c t", c=4), f"z_sb{n}")

                if A:
                    A.wait("xT_pe")
                    A.free("q_pe")
                    copy(xnT[:, :, :], bT[:, 0:256].rearrange("p (a t) -> p a t", a=2), "xT_sb")
                    A.wait("xT_pe")
                    A.free("v_pe")
                    copy(ctxT[:, :, :, :], bT[0:CTX, 256:384].rearrange("l (b k) -> l b k", b=2)
                         .unsqueeze(2).to_broadcast([CTX, 2, 2, SEQ]), "ctxT_sb")
                    A.wait("q_pe")
                    A.free("kdiag1")
                    copy(kT[:, :, :], bD[:, 256:512].rearrange("p (a t) -> p a t", a=2), "k_sb")
                if Fw:
                    up_bias(0)
                    up_tanh(0)
                if A:
                    A.wait("q_pe")
                    A.free("s_pe1")
                    copy(qT[:, :, :], bD[:, 0:256].rearrange("p (a t) -> p a t", a=2), "q_sb")
                    values(0)
                if Fw:
                    up_bias(1)
                if B:
                    B.wait("x1_ok")
                    B.free_dma_side(f"y_out{side}")
                    copy(x1k[:, side, :], x1[:, side, :], "x1k_ok")
                if Fw:
                    up_tanh(1)
                if A:
                    values(1)
                    exps(0)
                if Fw:
                    Fw.wait("hid_pe")
                    Fw.free("z_pe3")
                    nc.scalar.activation(hT[:, :], bD[:, 0:TILE], ACT.Identity, bias=bdn_sb[:, 0:1]).then_inc(S["hid_sb"], 1)
                if Ct:
                    Ct.wait("zp_ok")
                    nc.scalar.activation(zt[:, :], zp[:, :], ACT.Tanh, scale=0.5).then_inc(S["zt_ok"], 1)
                if Fw:
                    similarities(0)
                if A:
                    exps(1)
                if Fw:
                    similarities(1)
                    z_copy(0)
                if A:
                    probs_T(0)
                    probs_T(1)
                if Ct:
                    coef_copy(0)
                    coef_copy(1)
                if Fw:
                    z_copy(1)
                if Ct:
                    coef_copy(2)
                if A:
                    A.wait("oT_pe")
                    A.free("wo_pe")
                    copy(oT[:, :, :], bT[:, 0:256].rearrange("p (a t) -> p a t", a=2), "oT_sb")
                if Ct:
                    coef_copy(3)
                if B:
                    B.wait("top_i")
                    B.free("pick_ok")
                    copy(top_rep[:, :, :, :], topi[:, :, :].rearrange("p l a -> p a l").unsqueeze(3).to_broadcast([128, K8, 2 * RH, K8]), "rep_ok")
                    B.wait("dif_ok")
                    B.free("p_ok")
                    nc.scalar.activation(ex[:, :, :], dif[:, :, :], ACT.Exp).then_inc(S["ex_ok"], 1)
                if Fw:
                    z_copy(2)
                if A:
                    A.wait("x2T_pe")
                    A.free("up_pe1")
                    copy(xn2T[:, :, :], bT[:, 0:256].rearrange("p (a t) -> p a t", a=2), "x2T_sb")
                if Fw:
                    z_copy(3)
                if B:
                    B.wait("sm_pe")
                    B.free2("hotr3")
                    B.free2("hotc")
                    for half in range(2):
                        rows, cols = slice(half * 64, half * 64 + 64), slice(half * Q, half * Q + Q)
                        src = bG1[rows, 0:384].rearrange("p (n t) -> p n t", n=3)
                        nc.scalar.activation(rc_sm[rows, side, :, :], src[:, 0:2, cols], ACT.Copy)
                        last = nc.scalar.activation(p_sm[rows, side, :], src[:, 2, cols], ACT.Copy)
                    last.then_inc(S["sm_ok"], 1)

            act.wait_ge(S["small_in"], 64)
            nc.scalar.activation(gates[:, :], gates[:, :], ACT.Tanh).then_inc(S["gate_done"], 1)
            act.wait_ge(S["gate_done"], 1)
            nc.scalar.activation(gates[:, 1:2], gates[:, 1:2], ACT.Copy, scale=0.5).then_inc(S["gate_done"], 1)
            start(act, turn, 0)
            move_weights(act, 1, ATTENTION)
            start(act, turn, 1)
            move_weights(act, 1, OTHERS)
            act.wait_ge(S["simw_done"], 1)
            pipeline(act, turn)

        @block.vector
        def _(dve):
            def turn(L, A, Fw, B, Ct, side):
                cs = 1 - side

                def gathered(k):
                    Ct.wait(f"g_pe{k}")
                    Ct.wait("hotc")
                    if k < 2:
                        Ct.free(f"zs{k + 2}")
                    else:
                        Ct.wait(f"zs{k - 2}")
                    nc.vector.tensor_tensor(picked[:, k % 2, :, :], bG[k % 2][:, :].rearrange("s (q c) -> s q c", q=16),
                                            hot_c[:, :, 16 * k:16 * k + 16].rearrange("s c q -> s q c"), ALU.mult).then_inc(S[f"gm{k}"], 1)

                def gathered_sum(k):
                    Ct.wait(f"gm{k}")
                    nc.vector.tensor_reduce(zs[:, 16 * k:16 * k + 16], picked[:, k % 2, :, :], AX.X, ALU.add).then_inc(S[f"zs{k}"], 1)

                def hot_T(part):
                    qs = slice(part * Q // 2, (part + 1) * Q // 2)
                    Ct.wait_dma(f"rows_in{part}")
                    nc.vector.tensor_scalar(hot_rT[:, qs, :], hot_rT[:, qs, :], p_iota[:, 0:1], None, ALU.is_equal).then_inc(S[f"hotrT{part}"], 1)

                def hot_rows(k):
                    if k == 0:
                        Ct.wait("sm_ok")
                        Ct.free("w_pe3")
                    nc.vector.tensor_tensor(hot_r[:, :, 16 * k:16 * k + 16],
                                            rc_sm[:, cs, 0:1, 16 * k:16 * k + 16].to_broadcast([128, R, 16]),
                                            col_iota[:, :, :], ALU.is_equal).then_inc(S[f"hotr{k}"], 1)

                def coef_parts(n):
                    Ct.wait(f"uh{n + 1}")
                    Ct.free("w_pe3")
                    nc.vector.tensor_tensor(uc[:, n, :, :], hot_c[:, :, :],
                                            u_h[:, n:n + 1, :].to_broadcast([128, 2 * C, Q]), ALU.mult).then_inc(S[f"uc{n}"], 1)

                def scores_max(half):
                    hs = slice(8 * half, 8 * half + 8)
                    A.wait(f"s_pe{half}")
                    nc.vector.reduce_max(smax[:, hs], bS[half][:, :].rearrange("p (h k) -> p h k", h=8), AX.X).then_inc(S[f"max{half}"], 1)

                def scores_bias(half):
                    hs = slice(8 * half, 8 * half + 8)
                    A.wait(f"max{half}")
                    nc.vector.tensor_scalar(nbias[:, hs], smax[:, hs], -(HD ** -0.5), None, ALU.mult).then_inc(S[f"nb{half}"], 1)

                def up_silu(n):
                    Fw.wait(f"tanh{n}")
                    nc.vector.scalar_tensor_tensor(up_act[:, 4 * n:4 * n + 4, :], up_t[:, 4 * n:4 * n + 4, :], 1.0,
                                                   up_pre[:, 4 * n:4 * n + 4, :], ALU.add, ALU.mult).then_inc(S[f"act{n}"], 1)

                av = bD[:, 0:8 * 2 * (HD + 1)].rearrange("q (h o d) -> q h o d", h=8, o=2)

                if B:
                    B.wait_apart("sim_sb1")
                    for l in range(2 * RH):
                        last = nc.vector.max(top[:, l, :], sims[:, side, l, :])
                    last.then_inc(S["top_v"], 1)
                if Ct:
                    hot_rows(0)
                    Ct.wait("sm_ok")
                    nc.vector.tensor_tensor(
                        hot_c[:, :, :].rearrange("s c (a q) -> s a c q", q=16),
                        rc_sm[:, cs, 1, :].rearrange("s (a q) -> s a q", q=16).unsqueeze(2).to_broadcast([128, 4, 2 * C, 16]),
                        col_iota[:, 0:2 * C, :].unsqueeze(1).to_broadcast([128, 4, 2 * C, 16]), ALU.is_equal).then_inc(S["hotc"], 1)
                    hot_rows(1)
                    hot_T(0)
                    hot_rows(2)
                if Fw:
                    up_silu(0)
                if Ct:
                    gathered(0)
                    hot_T(1)
                    gathered_sum(0)
                    gathered(1)
                if A:
                    scores_max(0)
                if Fw:
                    up_silu(1)
                if Ct:
                    gathered_sum(1)
                if A:
                    scores_bias(0)
                if Ct:
                    gathered(2)
                    gathered(3)
                    gathered_sum(2)
                    gathered_sum(3)
                    Ct.wait("zs3")
                    nc.vector.tensor_tensor(zp[:, :], zs[:, :], p_sm[:, cs, :], ALU.mult).then_inc(S["zp_ok"], 1)
                if A:
                    scores_max(1)
                if Ct:
                    Ct.wait("zt_ok")
                    nc.vector.scalar_tensor_tensor(u[:, :], zt[:, :], 1.0, zp[:, :], ALU.add, ALU.mult).then_inc(S["u_ok"], 1)
                if A:
                    scores_bias(1)
                if Ct:
                    Ct.wait("u_ok")
                    nc.vector.tensor_copy(u_h[:, 0, :], u[:, :]).then_inc(S["uh1"], 1)
                    Ct.wait("uh1")
                    nc.vector.tensor_tensor(u_l[:, :], u[:, :], u_h[:, 0, :], ALU.subtract).then_inc(S["ul_ok"], 1)
                    Ct.wait("ul_ok")
                    nc.vector.tensor_copy(u_h[:, 1, :], u_l[:, :]).then_inc(S["uh2"], 1)
                if B:
                    B.wait("top_v")
                    nc.vector.tensor_tensor(sums[:, :, :, :],
                                            top[:, 0:RH, :].unsqueeze(3).to_broadcast([128, RH, K8, K8]),
                                            top[:, RH:2 * RH, :].unsqueeze(2).to_broadcast([128, RH, K8, K8]), ALU.add).then_inc(S["sums_ok"], 1)
                if Ct:
                    Ct.wait("uh2")
                    nc.vector.tensor_tensor(u_h[:, 2, :], u_l[:, :], u_h[:, 1, :], ALU.subtract).then_inc(S["uh3"], 1)
                    coef_parts(0)
                    coef_parts(1)
                    coef_parts(2)
                if B:
                    B.wait_apart("sums_ok")
                    for h in range(RH):
                        last = nc.vector.max(best[:, h, :], sums[:, h, :, :].rearrange("p a b -> p (a b)"))
                    last.then_inc(S["best_v"], 1)
                if A:
                    A.wait("av_pe")
                    nc.vector.reciprocal(rsum[:, :, :, :], av[:, :, :, HD:HD + 1]).then_inc(S["rs_ok"], 1)
                if B:
                    B.wait_apart("best_v")
                    for h in range(RH):
                        last = nc.vector.max_index(besti[:, h, :], best[:, h, :], sums[:, h, :, :].rearrange("p a b -> p (a b)"))
                    last.then_inc(S["best_i"], 1)
                if A:
                    A.wait("rs_ok")
                    A.free("x2T_pe")
                    nc.vector.tensor_tensor(xn[:, :].rearrange("q (h o d) -> q h o d", h=8, o=2), av[:, :, :, 0:HD],
                                            rsum[:, :, :, :].to_broadcast([128, 8, 2, HD]), ALU.mult).then_inc(S["o_ok"], 1)
                if Ct:
                    hot_rows(3)
                if B:
                    B.wait("best_i")
                    nc.vector.tensor_scalar(ab_i[:, 0, :], besti[:, :, :].rearrange("p h k -> p (h k)"), 3, None,
                                            ALU.logical_shift_right)
                    nc.vector.tensor_scalar(ab_i[:, 1, :], besti[:, :, :].rearrange("p h k -> p (h k)"), 7, None,
                                            ALU.bitwise_and).then_inc(S["b_ok"], 1)
                    B.wait("b_ok")
                    nc.vector.tensor_copy(ab_h[:, :], ab_i[:, :, :].rearrange("p a s -> p (a s)")).then_inc(S["ab_ok"], 1)
                    B.wait_apart("top_v")
                    for l in range(2 * RH):
                        last = nc.vector.max_index(topi[:, l, :], top[:, l, :], sims[:, side, l, :])
                    last.then_inc(S["top_i"], 1)
                if L:
                    L.wait_dma_side(f"x_in{1 - side}")
                    nc.vector.bn_stats(st6[:, :], xt[:, 1 - side, :]).then_inc(S["stats"], 1)
                if B:
                    B.wait("ab_ok")
                    nc.vector.tensor_tensor(eq[:, :, :], ab_h[:, :].unsqueeze(1).to_broadcast([128, K8, 2 * SLOTS]),
                                            a_iota[:, :, :], ALU.is_equal).then_inc(S["eq_ok"], 1)
                    B.wait("eq_ok")
                    B.wait("rep_ok")
                    nc.vector.tensor_tensor(eq[:, :, :], eq[:, :, :], top_rep[:, :, :, :].rearrange("p a l k -> p a (l k)"),
                                            ALU.mult).then_inc(S["pick_ok"], 1)
                if A:
                    A.wait("wo_pe")
                    A.free2("x1k_ok")
                    nc.vector.scalar_tensor_tensor(x1[:, side, :], bD[:, 0:DM], gates[:, 0:1], xt[:, side, :],
                                                   ALU.mult, ALU.add).then_inc(S["x1_ok"], 1)
                if B:
                    B.wait("pick_ok")
                    nc.vector.tensor_tensor(eq[:, 0:4, :], eq[:, 0:4, :], eq[:, 4:8, :], ALU.add).then_inc(S["tree4"], 1)
                if L:
                    L.wait_apart("stats")
                    nc.vector.bn_aggr(mv[:, :], st6[:, :]).then_inc(S["stats2"], 1)
                if B:
                    B.wait("tree4")
                    nc.vector.tensor_tensor(eq[:, 0:2, :], eq[:, 0:2, :], eq[:, 2:4, :], ALU.add).then_inc(S["tree2"], 1)
                    B.wait("tree2")
                    nc.vector.tensor_tensor(xy[:, :, :].rearrange("p a s -> p (a s)"), eq[:, 0, :], eq[:, 1, :], ALU.add).then_inc(S["xy_ok"], 1)
                    B.wait("best_v")
                    B.free("ex_ok")
                    nc.vector.tensor_tensor(dif[:, :, :], best[:, :, :], best[:, :, 0:1].to_broadcast([128, RH, K8]),
                                            ALU.subtract).then_inc(S["dif_ok"], 1)
                    B.wait("xy_ok")
                    nc.vector.scalar_tensor_tensor(e_i[:, :], xy[:, 0, :], float(NK), xy[:, 1, :], ALU.mult, ALU.add).then_inc(S["e_ok"], 1)
                    B.wait("e_ok")
                    nc.vector.tensor_scalar(rc_i[:, 0, :], e_i[:, :], R - 1, None, ALU.bitwise_and)
                    nc.vector.tensor_scalar(rc_i[:, 1, :], e_i[:, :], R.bit_length() - 1, None,
                                            ALU.logical_shift_right).then_inc(S["rci_ok"], 1)
                    B.wait("rci_ok")
                    B.free("rows_out", 32)
                    nc.vector.tensor_copy(r_h[:, :], rc_i[:, 0, :]).then_inc(S["rh_ok"], 1)
                if L:
                    L.wait("stats2")
                    nc.vector.tensor_scalar(veps[:, :], mv[:, 1:2], EPS, None, ALU.add).then_inc(S["eps_ok"], 1)
                if B:
                    B.wait("ex_ok")
                    nc.vector.reduce_sum(exs[:, :, 0], ex[:, :, :], AX.X).then_inc(S["exs_ok"], 1)
                    B.wait("exs_ok")
                    nc.vector.reciprocal(exr[:, :, :], exs[:, :, :]).then_inc(S["exr_ok"], 1)
                if A:
                    A.wait("x1_ok")
                    nc.vector.bn_stats(st6b[:, :], x1[:, side, :]).then_inc(S["lstats"], 1)
                if B:
                    B.wait("rci_ok")
                    B.free("sm_pe")
                    nc.vector.tensor_copy(sm_in[:, 0, :, :], rc_i[:, 0:1, :].to_broadcast([128, 2, SLOTS]))
                    nc.vector.tensor_copy(sm_in[:, 1, 0, :], rc_i[:, 1, :])
                    nc.vector.tensor_scalar(sm_in[:, 1, 1, :], rc_i[:, 1, :], float(C), None, ALU.add).then_inc(S["rdup_ok"], 1)
                if A:
                    A.wait_apart("lstats")
                    nc.vector.bn_aggr(mvb[:, :], st6b[:, :]).then_inc(S["lstats2"], 1)
                    A.wait("lstats2")
                    nc.vector.tensor_scalar(vepsb[:, :], mvb[:, 1:2], EPS, None, ALU.add).then_inc(S["leps_ok"], 1)
                if B:
                    B.wait("exr_ok")
                    B.free("sm_pe")
                    for half in range(2):
                        last = nc.vector.tensor_tensor(sm_in[:, 2, half, :].rearrange("p (h k) -> p h k", h=RH), ex[:, :, :],
                                                       exr[:, :, :].to_broadcast([128, RH, K8]), ALU.mult)
                    last.then_inc(S["p_ok"], 1)
                if A:
                    A.wait("lrstd_ok")
                    A.wait("oT_pe")
                    nc.vector.tensor_scalar(xn[:, :], x1[:, side, :], mvb[:, 0:1], rstdb[:, 0:1],
                                            ALU.subtract, ALU.mult).then_inc(S["xn2_ok"], 1)
                if L:
                    L.wait("rstd_ok")
                    L.free("xT_pe")
                    nc.vector.tensor_scalar(xn1[:, :], xt[:, 1 - side, :], mv[:, 0:1], rstd[:, 0:1], ALU.subtract, ALU.mult).then_inc(S["xn_ok"], 1)
                if Ct:
                    Ct.wait("out_pe")
                    Ct.wait("x1k_ok")
                    nc.vector.scalar_tensor_tensor(x1k[:, cs, :], bG0[:, 0:DM], gates[:, 1:2], x1k[:, cs, :],
                                                   ALU.mult, ALU.add).then_inc(S["y_ok"], 1)

            start(dve, turn, 0)
            move_weights(dve, 0, ATTENTION)
            dve.wait_ge(S["gate_done"], 2)
            start(dve, turn, 1)
            move_weights(dve, 0, OTHERS)
            dve.wait_ge(S["simw_pe"], 1)
            for s in range(2):
                last = nc.vector.tensor_copy(simW[:, s, :], banks[s][:, 0:RH * NK])
            last.then_inc(S["simw_done"], 1)
            dve.wait_ge(S["consts"], 2)
            pipeline(dve, turn)

        @block.tensor
        def _(pe):
            mm = nc.tensor.matmul
            def turn(L, A, Fw, B, Ct, side):
                cs = 1 - side

                def gather(k):
                    if k % 2 == 0:
                        Ct.wait(f"hotrT{k // 2}")
                    if k == 0:
                        Ct.wait("zll_ok")
                        Ct.free("y_ok")
                    elif k == 1:
                        Ct.wait("sm_ok")
                    if k >= 2:
                        Ct.wait(f"gm{k - 2}")
                    parts = [zz[:, cs, :, :].bitcast(H)[:, :, 1::2] for zz in (z, zl)] + [zll[:, cs, :, :]]
                    for q in range(16 * k, 16 * k + 16):
                        for n, part in enumerate(parts):
                            last = mm(bG[k % 2][:, 32 * (q - 16 * k):32 * (q - 16 * k) + 32], hot_rT[:, q, :],
                                      part.rearrange("r c (h q) -> r h c q", h=2)[:, :, :, q], start=(n == 0), stop=(n == 2))
                    last.then_inc(S[f"g_pe{k}"], 1)

                def scatter(k):
                    if k == 0:
                        for n in range(3):
                            Ct.wait(f"uc{n}")
                    Ct.wait(f"hotr{k}")
                    Ct.wait(f"gm{k + 2}" if k < 2 else f"w_sb{k - 2}")
                    for q in range(16 * k, 16 * k + 16):
                        for n in range(3):
                            last = mm(bG[k % 2][:, 32 * (q - 16 * k):32 * (q - 16 * k) + 32], hot_r[:, :, q], uc[:, n, :, q],
                                      start=(n == 0), stop=(n == 2))
                    last.then_inc(S[f"w_pe{k}"], 1)

                def up(n):
                    Fw.wait("x2T_sb")
                    Fw.free(f"z_sb{2 + n}")
                    for m in range(4):
                        c = 4 * n + m
                        for k in range(2):
                            last = mm(bS[n][:, 128 * m:128 * m + 128], WupT[:, k, 128 * c:128 * c + 128], xn2T[:, k, :],
                                      start=(k == 0), stop=(k == 1))
                    last.then_inc(S[f"up_pe{n}"], 1)

                def scores(half):
                    A.wait("q_sb")
                    if Fw:
                        Fw.wait(f"pre{half}")
                    mm(bS[half][:, :], ident_h[:, :], causal[:, :, :].rearrange("p h k -> p (h k)"), start=True, stop=False)
                    A.wait(f"kdiag{half}")
                    for s in range(2):
                        last = mm(bS[half][64 * s:64 * s + 64, :], qT[:, half, 64 * s:64 * s + 64],
                                  k_diag[:, half, s, :, :].rearrange("p h k -> p (h k)"), start=False, stop=True)
                    last.then_inc(S[f"s_pe{half}"], 1)

                def dense(n):
                    Fw.wait("hid_sb")
                    if n >= 2:
                        Fw.wait(f"z_sb{n - 2}")
                    elif A:
                        A.wait(f"exp{n}")
                    for m in range(4):
                        c = 4 * n + m
                        last = mm(bS[n % 2][:, 128 * m:128 * m + 128], deT[:, R * c:R * c + R], hT[:, :], start=True, stop=True)
                    last.then_inc(S[f"z_pe{n}"], 1)

                def similarity(s):
                    Fw.wait("hid_sb")
                    if s == 0 and A:
                        A.wait("v_sb0")
                        A.wait("v_sb1")
                    if s == 1:
                        Fw.wait("pt_sb1")
                    mm(bP[s][:, 0:RH * NK], hT[:, :], simW[:, s, :], start=True, stop=True).then_inc(S[f"sim_pe{s}"], 1)

                def probs_T(n):
                    A.wait(f"exp{n}")
                    if Fw:
                        Fw.wait(f"sim_sb{n}")
                    for j in range(4):
                        hp = 4 * n + j
                        last = nc.tensor.transpose(bP[n][:, 128 * j:128 * j + 128],
                                                   P[:, 2 * hp:2 * hp + 2, :].rearrange("p h k -> p (h k)"), ident[:, :])
                    last.then_inc(S[f"pt_pe{n}"], 1)

                if A:
                    A.wait("xn_ok")
                    A.wait_dma_side(f"ctx_in{side}")
                    A.free("x2T_sb")
                    for k in range(2):
                        nc.tensor.transpose(bT[:, 128 * k:128 * k + 128], xn1[:, 128 * k:128 * k + 128], ident[:, :])
                    nc.tensor.transpose(bT[0:CTX, 256:384], ct[:, side, :], ident[:, :]).then_inc(S["xT_pe"], 1)
                if Fw:
                    up(0)
                if A:
                    A.wait("xT_sb")
                    A.wait("ctxT_sb")
                    A.free("x1_ok")
                    for m in range(2):
                        mm(bD[:, 256 + 128 * m:384 + 128 * m], WkvT[:, 128 * m:128 * m + 128], ctxT[:, :, 0, :], start=True, stop=True)
                    for m in range(2):
                        for k in range(2):
                            last = mm(bD[:, 128 * m:128 * m + 128], WqT[:, k, 128 * m:128 * m + 128], xnT[:, k, :], start=(k == 0), stop=(k == 1))
                    last.then_inc(S["q_pe"], 1)
                if Fw:
                    up(1)
                if A:
                    A.free("pt_sb0")
                    A.wait("ctxT_sb")
                    for s in range(2):
                        last = mm(bP0[:, 256 * s:256 * s + 256], ctxT[:, s, :, :].rearrange("l d k -> l (d k)"), WkvT[:, DM:2 * DM],
                                  start=True, stop=True)
                    last.then_inc(S["v_pe"], 1)
                if Ct:
                    gather(0)
                if A:
                    scores(0)
                if Ct:
                    gather(1)
                    gather(2)
                    gather(3)
                if Fw:
                    if A:
                        A.wait("q_sb")
                    for c in range(DUP // 128):
                        if c % 4 == 0:
                            Fw.wait(f"act{c // 4}")
                        last = mm(bD[:, 0:TILE], WdT[:, c, :], up_act[:, c, :], start=(c == 0), stop=(c == DUP // 128 - 1))
                    last.then_inc(S["hid_pe"], 1)
                if A:
                    scores(1)
                if Fw:
                    similarity(0)
                    similarity(1)
                if A:
                    probs_T(0)
                if Fw:
                    dense(0)
                    dense(1)
                if A:
                    probs_T(1)
                if Fw:
                    dense(2)
                if A:
                    A.wait("pt_sb0")
                    A.wait("pt_sb1")
                    A.wait("v_sb1")
                    A.wait("q_sb")
                    if Fw:
                        Fw.wait("hid_sb")
                    for s in range(2):
                        for hp in range(8):
                            last = mm(bD[64 * s:64 * s + 64, 34 * hp:34 * hp + 34], PT[:, hp, 64 * s:64 * s + 64],
                                      v_diag[:, s, hp, :, :].rearrange("p o d -> p (o d)"), start=True, stop=True)
                    last.then_inc(S["av_pe"], 1)
                if Ct:
                    scatter(0)
                    scatter(1)
                    scatter(2)
                if A:
                    A.wait("o_ok")
                    for k in range(2):
                        last = nc.tensor.transpose(bT[:, 128 * k:128 * k + 128], xn[:, 128 * k:128 * k + 128], ident[:, :])
                    last.then_inc(S["oT_pe"], 1)
                if Ct:
                    scatter(3)
                if A:
                    A.wait("oT_sb")
                    for k in range(2):
                        last = mm(bD[:, 0:DM], oT[:, k, :], WoT[:, k, :], start=(k == 0), stop=(k == 1))
                    last.then_inc(S["wo_pe"], 1)
                if Ct:
                    Ct.wait("w_sb3")
                    for c in range(C):
                        last = mm(bG0[:, 0:DM], coef[:, c, :, :].rearrange("r h q -> r (h q)"), ue[:, c, :], start=(c == 0), stop=(c == C - 1))
                    last.then_inc(S["out_pe"], 1)
                if A:
                    A.wait("xn2_ok")
                    A.wait("oT_sb")
                    for k in range(2):
                        last = nc.tensor.transpose(bT[:, 128 * k:128 * k + 128], xn[:, 128 * k:128 * k + 128], ident[:, :])
                    last.then_inc(S["x2T_pe"], 1)
                if B:
                    B.wait("rdup_ok")
                    B.wait("p_ok")
                    if Ct:
                        Ct.wait("w_sb3")
                    for n in range(3):
                        last = nc.tensor.transpose(bG1[:, 128 * n:128 * n + 128], sm_in[:, n, :, :].rearrange("p a s -> p (a s)"), ident[:, :])
                    last.then_inc(S["sm_pe"], 1)
                if Fw:
                    dense(3)

            groups = list(weight_groups())

            def transpose_weights(numbers):
                for n in numbers:
                    arrived, transfers, srcs, dst, scale = groups[n]
                    pe.wait_ge(S[arrived], 16 * transfers)
                    if n >= 8:
                        pe.wait_ge(S["wT_act" if n % 2 else "wT_dve"], (n - 8) // 2 + 1)
                    for j, s in enumerate(srcs):
                        rows = s.shape[0]
                        last = nc.tensor.transpose(banks[n % 8][0:s.shape[1], 128 * j:128 * j + rows], s, ident[0:rows, 0:rows])
                    last.then_inc(S["wT_pe"], 1)

            pe.wait_ge(S["ident_ok"], 1)
            transpose_weights(ATTENTION)
            pe.wait_ge(S["wT_dve"], 2)
            pe.wait_ge(S["wT_act"], 1)
            pe.wait_ge(S["consts"], 1)
            start(pe, turn, 1)
            pe.wait_ge(S["x2T_sb"], 1)
            transpose_weights(OTHERS)
            pe.wait_ge(S["wT_dve"], (len(groups) + 1) // 2)
            pe.wait_ge(S["wT_act"], len(groups) // 2)
            for s in range(2):
                rows = slice(64 * s, 64 * s + 64)
                for h in range(RH):
                    last = mm(banks[s][:, NK * h:NK * h + NK], wr_n[rows, h, :], keysT[rows, h, :], start=True, stop=True)
            last.then_inc(S["simw_pe"], 1)
            pe.wait_ge(S["simw_done"], 1)
            pe.wait_ge(S["ue_in"], 16)
            pipeline(pe, turn)


_INS = ["x", "ctx_512", "g_xattn", "g_ffn", "L0_xattn_Wq", "L0_xattn_Wkv_expand", "L0_xattn_Wout", "L0_ffn_W_up",
        "L0_ffn_b_up", "L0_ffn_W_down", "L0_ffn_b_down", "L0_ffn_W_q", "L0_ffn_keys", "L0_ffn_down_embed",
        "L0_ffn_up_embed"]


def kernel(**inputs):
    import numpy as _np
    import concourse.bacc as _bacc
    from concourse import mybir as _mybir
    from concourse.bass_utils import run_bass_kernel_spmd as _run

    nc = _bacc.Bacc("TRN2", target_bir_lowering=False, num_devices=1)
    arrays, args = {}, []
    for name in _INS:
        a = _np.ascontiguousarray(inputs[name])
        arrays[f"in_{name}"] = a
        args.append(nc.dram_tensor(f"in_{name}", a.shape, _mybir.dt.from_np(a.dtype), kind="ExternalInput").ap())
    args.append(nc.dram_tensor("out", (64, 64, 256), _mybir.dt.float32, kind="ExternalOutput").ap())
    flamingo_layer(nc, *args)
    r = _run(nc, [arrays], core_ids=[0])
    return r.results[0]["out"]
```
